# Optimizing a Trainium2 kernel written in Bass

```python
import numpy as np
import jax
import jax.numpy as jnp

def _softmax(x, axis=-1):
    return jax.nn.softmax(x, axis=axis)

def _gelu(x):
    return jax.nn.gelu(x, approximate=True)

def _silu(x):
    return jax.nn.silu(x)

def _sigmoid(x):
    return jax.nn.sigmoid(x)

def _layernorm(x, axis=-1, eps=1e-05):
    m = jnp.mean(x, axis=axis, keepdims=True)
    v = jnp.var(x, axis=axis, keepdims=True)
    return (x - m) / jnp.sqrt(v + eps)

def _scatter_add(tgt, idx, src, axis=0):
    return tgt.at[idx].add(src)

def _segment_sum(src, seg, n):
    return jax.ops.segment_sum(src, seg, n)
kernel_name = 'mk_sandwich_d1_jaxref_r4_2db92d'

def setup_inputs(seed: int=0):
    np.random.seed(seed)
    _w = jnp.asarray

    def _L0_attn_setup():
        import jax, jax.numpy as jnp
        import numpy as np
        DIM = 256
        EPS = 1e-05

        def _layernorm(x, w, b):
            mu = jnp.mean(x, axis=-1, keepdims=True)
            var = jnp.mean(jnp.square(x - mu), axis=-1, keepdims=True)
            return (x - mu) * jax.lax.rsqrt(var + EPS) * w + b
        key = jax.random.key(seed)
        ks = jax.random.split(key, 7)
        C = DIM
        x = jax.random.normal(ks[0], (4, 1024, C), dtype=jnp.float32)
        norm_w = jnp.ones((C,), dtype=jnp.float32)
        norm_b = jnp.zeros((C,), dtype=jnp.float32)
        s = 1.0 / np.sqrt(C)
        qkv_w = jax.random.uniform(ks[1], (3 * C, C), dtype=jnp.float32, minval=-s, maxval=s)
        qkv_b = jax.random.uniform(ks[2], (3 * C,), dtype=jnp.float32, minval=-s, maxval=s)
        proj_w = jax.random.uniform(ks[3], (C, C), dtype=jnp.float32, minval=-s, maxval=s)
        proj_b = jax.random.uniform(ks[4], (C,), dtype=jnp.float32, minval=-s, maxval=s)
        return {'x': x, 'norm_w': norm_w, 'norm_b': norm_b, 'qkv_w': qkv_w, 'qkv_b': qkv_b, 'proj_w': proj_w, 'proj_b': proj_b}
    _L0_attn_in = _L0_attn_setup()

    def _L0_ffn_setup():
        import jax, jax.numpy as jnp
        import numpy as np
        B, M, D = (4, 512, 256)
        N, P = (64, 32)
        key = jax.random.key(seed)
        k1, k2, k3, k4 = jax.random.split(key, 4)
        x = jax.random.normal(k1, (B, M, D), dtype=jnp.float32)
        phi = jax.random.normal(k2, (D, N, P), dtype=jnp.float32) * (1.0 / np.sqrt(D))
        W = jax.random.normal(k3, (N, D, D), dtype=jnp.float32) * (1.0 / np.sqrt(D))
        b = jax.random.normal(k4, (N, D), dtype=jnp.float32) * 0.01
        return {'x': x, 'phi': phi, 'W': W, 'b': b}
    _L0_ffn_in = _L0_ffn_setup()
    _d = {'L0_attn_x': _L0_attn_in['x'], 'L0_attn_norm_w': _L0_attn_in['norm_w'], 'L0_attn_norm_b': _L0_attn_in['norm_b'], 'L0_attn_qkv_w': _L0_attn_in['qkv_w'], 'L0_attn_qkv_b': _L0_attn_in['qkv_b'], 'L0_attn_proj_w': _L0_attn_in['proj_w'], 'L0_attn_proj_b': _L0_attn_in['proj_b'], 'L0_ffn_phi': _L0_ffn_in['phi'], 'L0_ffn_W': _L0_ffn_in['W'], 'L0_ffn_b': _L0_ffn_in['b']}
    _x0 = _d['L0_attn_x']
    _d['L0_attn_x'] = jax.random.normal(jax.random.fold_in(jax.random.key(seed), 1), (2, 2048, 256), dtype=_x0.dtype)
    del _x0
    return _d

def reference(L0_attn_x, L0_attn_norm_w, L0_attn_norm_b, L0_attn_qkv_w, L0_attn_qkv_b, L0_attn_proj_w, L0_attn_proj_b, L0_ffn_phi, L0_ffn_W, L0_ffn_b):

    def _L0_attn_ref(x, norm_w, norm_b, qkv_w, qkv_b, proj_w, proj_b):
        import jax, jax.numpy as jnp
        import numpy as np
        DIM = 256
        EPS = 1e-05

        def _layernorm(x, w, b):
            mu = jnp.mean(x, axis=-1, keepdims=True)
            var = jnp.mean(jnp.square(x - mu), axis=-1, keepdims=True)
            return (x - mu) * jax.lax.rsqrt(var + EPS) * w + b
        B, T, C = x.shape
        residual = x
        h = _layernorm(x, norm_w, norm_b)
        qkv = jnp.einsum('btc,oc->bto', h, qkv_w) + qkv_b
        q, k, v = (qkv[..., :C], qkv[..., C:2 * C], qkv[..., 2 * C:])
        attn = jnp.einsum('btc,bsc->bts', q, k) / jnp.sqrt(jnp.float32(C))
        o = jnp.einsum('bts,bsc->btc', attn, v)
        o = jnp.einsum('btc,oc->bto', o, proj_w) + proj_b
        return residual + o

    def _L0_ffn_ref(x, phi, W, b):
        import jax, jax.numpy as jnp
        import numpy as np
        B, M, D = (4, 512, 256)
        N, P = (64, 32)
        logits = jnp.einsum('bmd,dnp->bmnp', x, phi)
        dispatch = jax.nn.softmax(logits, axis=0)
        bsz, m, n, p = logits.shape
        combine = jax.nn.softmax(logits.reshape(bsz, m, n * p), axis=-1).reshape(bsz, m, n, p)
        slots = jnp.einsum('bmd,bmnp->bnpd', x, dispatch)
        y = jnp.einsum('bnpd,nde->bnpe', slots, W) + b[None, :, None, :]
        out = jnp.einsum('bnpd,bmnp->bmd', y, combine)
        return out
    x = L0_attn_x
    x = x + _layernorm(_L0_attn_ref(_layernorm(x, axis=-1), L0_attn_norm_w, L0_attn_norm_b, L0_attn_qkv_w, L0_attn_qkv_b, L0_attn_proj_w, L0_attn_proj_b), axis=-1)
    x = x + _layernorm(_L0_ffn_ref(_layernorm(x, axis=-1), L0_ffn_phi, L0_ffn_W, L0_ffn_b), axis=-1)
    return x

_drawn_inputs = setup_inputs


def setup_inputs(seed=0):
    import zlib

    import numpy as np

    out = dict(_drawn_inputs(seed))
    spreads = {'L0_attn_norm_w': (1.0, 0.2), 'L0_attn_norm_b': (0.0, 0.1)}
    factors = {'L0_attn_proj_b': 8.0, 'L0_ffn_b': 8.0}
    for name, (base, spread) in spreads.items():
        noise = np.random.default_rng([zlib.crc32(name.encode()), seed]).standard_normal(out[name].shape)
        drawn = base * np.exp(spread * noise) if base else spread * noise
        out[name] = jnp.asarray(drawn.astype(out[name].dtype))
    for name, factor in factors.items():
        out[name] = (out[name] * factor).astype(out[name].dtype)
    return out
```

```python
import math
from contextlib import ExitStack

import concourse.bass as bass
from concourse import mybir

F32 = mybir.dt.float32
F16 = mybir.dt.float16
I32 = mybir.dt.int32
ALU = mybir.AluOpType
ACT = mybir.ActivationFunctionType
AX_X = mybir.AxisListType.X

P = 128
EPS = 1e-5
X_SCALE = 2.0 ** 10
S_SCALE = 2.0 ** 12
E_LOG = 14 * math.log(2.0)
TOP_EXP = 13


class Arena:

    def __init__(self, tensor, words):
        self.tensor, self.words, self.at = tensor, words, 0

    def take(self, words, dtype=F32, rows=P):
        assert self.at + words <= self.words, (self.at, words, self.words)
        view = self.tensor[0:rows, self.at:self.at + words]
        self.at += words
        return view if dtype == F32 else view.bitcast(dtype)


PASSED = []


def wait_apart(eng, sem, value):
    eng.wait_ge(sem, value)
    eng.sem_inc(PASSED[0], 1)


class Count:

    def __init__(self, eng, sem):
        self.eng, self.sem, self.base, self.n = eng, sem, 0, 0

    def add(self, ins):
        ins.then_inc(self.sem, 1)
        self.n += 1
        return ins

    def wait(self):
        self.eng.wait_ge(self.sem, self.base + self.n)

    def wait_apart(self):
        wait_apart(self.eng, self.sem, self.base + self.n)

    def enter(self, i, per):
        self.outer = (self.base, self.n, per)
        self.base, self.n = self.base + self.n + i * per, 0

    def leave(self, turns):
        base, n, per = self.outer
        assert self.n == per, (self.n, per)
        self.base, self.n = base + n + turns * per, 0


def build(nc, x, norm_w, norm_b, qkv_w, qkv_b, proj_wT, proj_b, phi, ffn_w, ffn_bT, out):
    B, T, C = x.shape
    N, D, _ = ffn_w.shape
    NP = phi.shape[1] * phi.shape[2]
    Q = phi.shape[2]
    NJ = T // P
    K = C // P
    KS = 3 * K
    NB = NP // 512
    NT = NP // P
    TB = 512 // P
    EP = P // Q
    GJ = 4
    NG = NJ // GJ
    assert (B, K, TB) == (2, 2, 4)

    x_v = x.rearrange("b (p j) c -> p b j c", j=NJ)
    out_v = out.rearrange("b (p j) c -> p b j c", j=NJ)
    phi_v = phi.rearrange("(k p) n q -> p k (n q)", p=P)
    w_v = ffn_w.rearrange("(t n) (k p) e -> t p n k e", n=EP, p=P)
    d_dram = nc.dram_tensor("logit_difference", [NJ, P, NP], F32, kind="Internal").ap()

    with ExitStack() as ctx:
        def sb(name, shape, dt=F32):
            return ctx.enter_context(nc.sbuf_tensor(name, shape, dt))

        def sem(name):
            return ctx.enter_context(nc.semaphore(name))

        xres = sb("xres", [P, B, NJ, C])
        phs = sb("phs", [P, 2, K, NP], F16)
        xT1 = sb("xT1", [P, 2, K, T], F16)
        ident = sb("ident", [P, P])
        ones = sb("ones", [1, P])
        tcount = sb("tcount", [1, 1])
        epst = sb("epst", [P, 4])
        A_sb = sb("A_sb", [P, B, K, C])
        abc = sb("abc", [P, B, C])
        bT = sb("bT", [P, K, N])
        stat = sb("stat", [P, 8, 6])
        small = sb("small", [P, 384])
        r_xdT = sb("r_xdT", [P, K * T])
        r_xn = sb("r_xn", [P, B * NJ * C])
        r_y = sb("r_y", [P, B * NT * C])
        r_1 = sb("r_1", [P, 6144])
        r_2 = sb("r_2", [P, 4096 + 2048 + 512])

        xdT = r_xdT[:, :].bitcast(F16).rearrange("p (h k t) -> p h k t", h=2, k=K)
        x3n = r_xn[:, :].bitcast(F16).rearrange("p (b j h c) -> p b j h c", b=B, j=NJ, h=2)
        yhl = r_xn[:, :].bitcast(F16).rearrange("p (b t h c) -> p b t h c", b=B, t=NT, h=2)
        yf = r_y[:, :].rearrange("p (b t c) -> p b t c", b=B, t=NT)

        a = Arena(r_xn, B * NJ * C)
        w_raw = a.take(KS * C).rearrange("p (s c) -> p s c", s=KS)
        w_aug = a.take(KS * (C + 1)).rearrange("p (s c) -> p s c", s=KS)
        wbc = a.take(C)
        bbc = a.take(C)
        junk = a.take(C)
        wpT = a.take(K * C).rearrange("p (k c) -> p k c", k=K)
        G = a.take(K * (C + 1)).rearrange("p (k c) -> p k c", k=K)
        g_row = a.take(C + 1, rows=1)
        u_row = a.take(C, rows=1)
        r_row = a.take(B * C, rows=1)
        c_row = a.take(B * C, rows=1)
        a_row = a.take(B * C, rows=1)
        pb2 = a.take(B * C, rows=1)
        a = Arena(r_y, B * NT * C)
        phf = a.take(K * NP).rearrange("p (k n) -> p k n", k=K)
        U = a.take(K * C).rearrange("p (k c) -> p k c", k=K)
        S_sb = a.take(B * K * (C + 1)).rearrange("p (b k c) -> p b k c", b=B, k=K)
        R = a.take(B * K * C).rearrange("p (b k c) -> p b k c", b=B, k=K)
        a = Arena(r_1, 6144)
        yb = a.take(GJ * B * C).rearrange("p (j b c) -> p j b c", j=GJ, b=B)
        x1a = a.take(GJ * B * C).rearrange("p (j b c) -> p j b c", j=GJ, b=B)
        x3f = a.take(GJ * B * C).rearrange("p (j b c) -> p j b c", j=GJ, b=B)
        a = Arena(r_2, 6656)
        Wt = a.take(4096).rearrange("p (w n k e) -> p w n k e", w=2, n=EP, k=K)
        xT = a.take(1024).rearrange("p (w c) -> p w c", w=2)
        xd = a.take(GJ * C).rearrange("p (j c) -> p j c", j=GJ)
        xbuf = sb("xbuf", [P, 4, C + 1])
        a = Arena(r_1, 6144)
        sF = a.take(2048).rearrange("p (w s n) -> p w s n", w=2, s=B)
        shl = a.take(2048, F16).rearrange("p (w h s n) -> p w h s n", w=2, h=2, s=B)
        dS = a.take(1024).rearrange("p (w n) -> p w n", w=2)
        a = Arena(r_2, 6656)
        a.take(4096)
        slT = a.take(2048).rearrange("p (k n b q) -> p k n b q", k=K, n=TB * EP, b=B)
        yT = a.take(512).rearrange("p (e b n) -> p e b n", e=K, b=B)
        a = Arena(r_1, 6144)
        E1, E0, l0 = a.take(2048), a.take(2048), a.take(2048)
        dB = r_xdT[:, 0:2048]
        a = Arena(r_2, 6656)
        eT = a.take(2048, F16).rearrange("p (w h m) -> p w h m", w=4, h=2)
        a = Arena(r_y, B * NT * C)
        c1 = a.take(512).rearrange("p (w c) -> p w c", w=2)
        u = a.take(512).rearrange("p (w c) -> p w c", w=2)
        fo = a.take(512).rearrange("p (w c) -> p w c", w=2)
        fz = a.take(512).rearrange("p (w c) -> p w c", w=2)

        sm = Arena(small, 384)
        bcol, qbc = sm.take(KS), sm.take(KS)
        mv = sm.take(16).rearrange("p (i s) -> p i s", s=2)
        mvx = sm.take(64).rearrange("p (b j s) -> p b j s", b=B, j=NJ)
        rx = sm.take(64).rearrange("p (s b j) -> p s b j", s=2, b=B)
        ve = sm.take(16)
        rr = sm.take(8)
        nm = sm.take(8)
        pm = sm.take(2)
        gm = sm.take(2)
        sg = sm.take(2)
        isg = sm.take(2)
        kap = sm.take(2)
        ymx = sm.take(NT)
        m4 = sm.take(8)
        m1 = sm.take(2)
        ebias = sm.take(2)
        zz = sm.take(4 * NJ).rearrange("p (w j s) -> p w j s", w=2, j=NJ)
        mvC = sm.take(4).rearrange("p (w s) -> p w s", w=2)
        tl = sm.take(16).rearrange("p (w s) -> p w s", w=2)

        psL = ctx.enter_context(nc.psum_tensor("psL", [P, 2048], F32))
        bk = [ctx.enter_context(nc.psum_tensor(f"bk{i}", [P, 512], F32)) for i in range(4)]

        par_loaded = sem("par_loaded")
        x_loaded = [sem(f"x_loaded{g}") for g in range(4)]
        phi_loaded = sem("phi_loaded")
        W_loaded = [sem(f"W_loaded{i}") for i in range(2)]
        pool_const = sem("pool_const")
        PASSED[:] = [sem("passed")]
        dve_own, pool_own = sem("dve_own"), sem("pool_own")
        waug_ready = sem("waug_ready")
        wprod_done, wprod_evac = sem("wprod_done"), sem("wprod_evac")
        stats_x, rstd_x = sem("stats_x"), sem("rstd_x")
        xh_ready, xh_used = sem("xh_ready"), sem("xh_used")
        S_evac = sem("S_evac")
        crow_done, crow_evac = sem("crow_done"), sem("crow_evac")
        R_done, R_evac = sem("R_done"), sem("R_evac")
        A_done, A_evac = sem("A_done"), sem("A_evac")
        arow_ready, abc_done, abc_ready = sem("arow_ready"), sem("abc_done"), sem("abc_ready")
        gmax_in, gmax_out = sem("gmax_in"), sem("gmax_out")
        phi_split = sem("phi_split")
        hT_done, hT_evac = sem("hT_done"), sem("hT_evac")
        y_done, y_read = sem("y_done"), sem("y_read")
        x1a_ready = sem("x1a_ready")
        mv_ready, r2_ready, z_ready, x2_ready = sem("mv_ready"), sem("r2_ready"), sem("z_ready"), sem("x2_ready")
        r3_ready, x3_ready, x3h_ready, x3l_ready = sem("r3_ready"), sem("x3_ready"), sem("x3h_ready"), sem("x3l_ready")
        xd_ready, x3T_done, x3Th_ready, x3Tl_ready = sem("xd_ready"), sem("x3T_done"), sem("x3Th_ready"), sem("x3Tl_ready")
        d_done, s_ready, d_copied, s_split, slots_used = (
            sem("d_done"), sem("s_ready"), sem("d_copied"), sem("s_split"), sem("slots_used"))
        d_stored = [sem(f"d_stored{i}") for i in range(2)]
        slots_evac = sem("slots_evac")
        yTp_done, yT_ready, yN_done, yN_evac = sem("yTp_done"), sem("yT_ready"), sem("yN_done"), sem("yN_evac")
        yh_ready, yl_ready = sem("yh_ready"), sem("yl_ready")
        l_done, m1_ready, m0_ready, E1_ready, E0_ready = (
            sem("l_done"), sem("m1_ready"), sem("m0_ready"), sem("E1_ready"), sem("E0_ready"))
        eT_done, eTh_ready, eTl_ready, comb_done = (
            sem("eT_done"), sem("eTh_ready"), sem("eTl_ready"), sem("comb_done"))
        c1_ready, u_ready, fin_ready = sem("c1_ready"), sem("u_ready"), sem("fin_ready")
        dB_loaded = sem("dB_loaded")
        out_stored = [sem(f"out_stored{i}") for i in range(2)]

        N_PAR = 8

        block = ctx.enter_context(nc.Block())

        @block.sync
        def _(sp):
            qw = qkv_w.rearrange("(s p) c -> p s c", p=P)
            sp.dma_start(w_raw, qw).then_inc(par_loaded, 16)
            sp.dma_start(wbc, norm_w.rearrange("(o c) -> o c", o=1).broadcast_to([P, C])).then_inc(par_loaded, 16)
            sp.dma_start(bbc, norm_b.rearrange("(o c) -> o c", o=1).broadcast_to([P, C])).then_inc(par_loaded, 16)
            for g in range(4):
                b, h = g // 2, g % 2
                sp.dma_start(xres[:, b, 8 * h:8 * h + 8, :], x_v[:, b, 8 * h:8 * h + 8, :]).then_inc(x_loaded[g], 16)
            sp.dma_start(phf, phi_v).then_inc(phi_loaded, 16)
            for w in range(2):
                sp.dma_start(Wt[:, w], w_v[w]).then_inc(W_loaded[w], 16)

            def block_io(nb, with_y):
                for j in range(NJ):
                    sp.wait_ge(d_copied, nb * NJ + (j + 3))
                    sp.dma_start(d_dram[j, :, bass.ds(nb * 512, 512)], dS[:, j % 2, :]).then_inc(d_stored[j % 2], 16)
                    if with_y and j % 4 == 3:
                        q = j // 4
                        sp.wait_ge(yTp_done, (nb - 1) * TB + (q + 1))
                        sp.dma_start(Wt[:, q % 2], w_v[bass.ds((nb - 1) * TB + (q + 2), 1)].rearrange(
                            "t p n k e -> p (t n) k e")).then_inc(W_loaded[q % 2], 16)

            block_io(0, False)
            with sp.Fori(1, NB) as nb:
                block_io(nb, True)
            for q in range(2):
                sp.wait_ge(yTp_done, (NB - 1) * TB + q + 1)
                sp.dma_start(Wt[:, q % 2], w_v[(NB - 1) * TB + q + 2]).then_inc(W_loaded[q % 2], 16)

            for i in range(2):
                sp.wait_ge(d_stored[i], 16 * (NB * NJ // 2 + 1))
            sp.wait_ge(slots_used, NB * NJ + 2)
            sp.dma_start(dB, d_dram[0]).then_inc(dB_loaded, 16)

            def store(b, j, fin):
                wait_apart(sp, fin_ready, fin + 2)
                w = 1 - b
                sp.dma_start(out_v[:, b, bass.ds(j, 1), :].rearrange("p j c -> p (j c)"),
                             fo[:, w, :]).then_inc(out_stored[w], 16)

            with sp.Fori(0, NJ - 1) as j:
                sp.wait_ge(m0_ready, j + 1)
                sp.dma_start(dB, d_dram[bass.ds(j + 1, 1)].rearrange("j p n -> p (j n)")).then_inc(dB_loaded, 16)
                store(1, j, 2 * j + 1)
                store(0, j, 2 * j + 2)
            store(1, NJ - 1, 2 * NJ - 1)
            store(0, NJ - 1, 2 * NJ)
            for i in range(2):
                sp.wait_ge(out_stored[i], 16 * (NJ + 1))

        @block.gpsimd
        def _(pool):
            own = Count(pool, pool_own)
            pool.sem_inc(fin_ready, 2)
            own.add(nc.gpsimd.memset(ident[:, :], 0.0))
            own.add(nc.gpsimd.memset(epst[:, 0:2], -0.5))
            own.add(nc.gpsimd.memset(epst[:, 2:3], -1.0))
            own.add(nc.gpsimd.memset(ones[:, :], 1.0))
            own.add(nc.gpsimd.memset(tcount[:, :], float(T)))
            own.wait()
            nc.gpsimd.affine_select(out=ident[:, :], in_=ident[:, :], compare_op=ALU.not_equal, fill=1.0,
                                    base=0, pattern=[[-1, P]], channel_multiplier=1).then_inc(pool_const, 1)

            def rsqrt(o, v):
                n = v.shape[1]
                return nc.gpsimd.tensor_tensor(o, v, epst[:, 0:1].broadcast_to([P, n]), ALU.pow)

            for g in range(4):
                b, h = g // 2, g % 2
                pool.wait_ge(stats_x, g + 1)
                va = ve.rearrange("p (s i) -> p s i", s=2)
                v = mvx[:, b, 8 * h:8 * h + 8, 1]
                own.add(nc.gpsimd.tensor_scalar(va[:, 0], v, EPS, 1.0, ALU.add, ALU.mult))
                own.wait_apart()
                own.add(nc.gpsimd.tensor_scalar(va[:, 1], va[:, 0], EPS, 0.0, ALU.mult, ALU.add))
                own.wait()
                own.add(nc.gpsimd.tensor_tensor(va[:, 1], va[:, 1], v, ALU.add))
                own.wait()
                own.add(rsqrt(rx[:, 0, b, 8 * h:8 * h + 8], va[:, 0]))
                rsqrt(rx[:, 1, b, 8 * h:8 * h + 8], va[:, 1]).then_inc(rstd_x, 1)
            pool.wait_ge(gmax_in, 1)
            nc.gpsimd.partition_all_reduce(gm[:, 0:1], pm[:, 0:1], P, bass.bass_isa.ReduceOp.max).then_inc(gmax_out, 1)

            pool.wait_ge(abc_ready, 1)

            with pool.Fori(0, NG) as g:
                own.enter(g, 9)
                gj = bass.ds(g * GJ, GJ)
                for b in range(B):
                    rs = rx[:, 0, b, gj].unsqueeze(2).broadcast_to([P, GJ, C])
                    me = mvx[:, b, gj, 0].unsqueeze(2).broadcast_to([P, GJ, C])
                    if b == 0:
                        wait_apart(pool, y_read, g * GJ + 2)
                    own.add(nc.gpsimd.tensor_tensor(x1a[:, :, b, :], xres[:, b, gj, :], me, ALU.subtract))
                    own.wait()
                    own.add(nc.gpsimd.tensor_tensor(x1a[:, :, b, :], x1a[:, :, b, :], rs, ALU.mult))
                    own.wait()
                    nc.gpsimd.tensor_tensor(x1a[:, :, b, :], x1a[:, :, b, :],
                                            abc[:, b:b + 1, :].broadcast_to([P, GJ, C]),
                                            ALU.add).then_inc(x1a_ready, 1)
                wait_apart(pool, mv_ready, 2 * g + 1)
                own.add(nc.gpsimd.tensor_scalar(ve[:, 0:8], mv[:, :, 1], EPS, 1.0, ALU.add, ALU.mult))
                own.wait()
                own.add(rsqrt(rr, ve[:, 0:8]))
                own.wait()
                own.add(nc.gpsimd.tensor_tensor(nm, mv[:, :, 0], rr, ALU.mult))
                own.wait_apart()
                nc.gpsimd.tensor_scalar(nm, nm, -1.0, 0.0, ALU.mult, ALU.add).then_inc(r2_ready, 1)
                wait_apart(pool, z_ready, g + 1)
                for b in range(B):
                    nc.gpsimd.tensor_tensor(xres[:, b, gj, :], xres[:, b, gj, :], yb[:, :, b, :],
                                            ALU.add).then_inc(x2_ready, 1)
                wait_apart(pool, mv_ready, 2 * g + 2)
                own.add(nc.gpsimd.tensor_scalar(ve[:, 0:8], mv[:, :, 1], EPS, 1.0, ALU.add, ALU.mult))
                own.wait()
                own.add(rsqrt(ve[:, 8:16], ve[:, 0:8]))
                own.wait_apart()
                nc.gpsimd.tensor_scalar(rr, ve[:, 8:16], X_SCALE, 0.0, ALU.mult, ALU.add).then_inc(r3_ready, 1)
                pool.wait_ge(x3_ready, g + 1)
                nc.gpsimd.tensor_tensor(xd, x3f[:, :, 0, :], x3f[:, :, 1, :], ALU.subtract).then_inc(xd_ready, 1)
                own.leave(NG)

            pool.wait_ge(gmax_in, 2)
            nc.gpsimd.partition_all_reduce(gm[:, 1:2], pm[:, 1:2], P, bass.bass_isa.ReduceOp.max).then_inc(gmax_out, 1)
            pool.wait_ge(gmax_in, 3)

            def finish(b, j, seq, n):
                w = 1 - b
                t = tl[:, w, :]
                pool.wait_ge(u_ready, seq + 3)
                own.add(nc.gpsimd.tensor_tensor(t[:, 0:1], zz[:, w, bass.ds(j, 1), 0], zz[:, w, bass.ds(j, 1), 1], ALU.add))
                own.wait()
                own.add(nc.gpsimd.tensor_tensor(t[:, 1:2], t[:, 0:1], epst[:, 2:3], ALU.pow))
                own.wait()
                own.add(nc.gpsimd.tensor_tensor(t[:, 2:3], t[:, 1:2], isg[:, 1:2], ALU.mult))
                own.wait()
                own.add(nc.gpsimd.tensor_tensor(t[:, 3:4], t[:, 2:3], mvC[:, w, 1:2], ALU.mult))
                own.wait()
                own.add(nc.gpsimd.tensor_tensor(t[:, 3:4], t[:, 3:4], t[:, 2:3], ALU.mult))
                own.wait_apart()
                own.add(nc.gpsimd.tensor_scalar(t[:, 3:4], t[:, 3:4], EPS, 1.0, ALU.add, ALU.mult))
                own.wait()
                own.add(rsqrt(t[:, 4:5], t[:, 3:4]))
                own.wait()
                own.add(nc.gpsimd.tensor_tensor(t[:, 5:6], t[:, 4:5], t[:, 2:3], ALU.mult))
                own.wait_apart()
                own.add(nc.gpsimd.tensor_scalar(fz[:, w, :], u[:, w, :], mvC[:, w, 0:1], t[:, 5:6],
                                                ALU.subtract, ALU.mult))
                own.wait()
                wait_apart(pool, out_stored[w], 16 * n + 16)
                nc.gpsimd.tensor_tensor(fo[:, w, :], fz[:, w, :],
                                        xres[:, b, bass.ds(j, 1), :].rearrange("p j c -> p (j c)"),
                                        ALU.add).then_inc(fin_ready, 1)

            finish(1, 0, 0, 0)
            with pool.Fori(1, NJ) as j:
                own.enter(j - 1, 18)
                finish(0, j - 1, 2 * j - 1, j - 1)
                finish(1, j, 2 * j, j)
                own.leave(NJ - 1)
            finish(0, NJ - 1, 2 * NJ - 1, NJ - 1)

        @block.scalar
        def _(act):
            act.dma_start(wpT, proj_wT.rearrange("(k p) e -> p k e", p=P)).then_inc(par_loaded, 16)
            act.dma_start(qbc, qkv_b).then_inc(par_loaded, 16)
            for b in range(B):
                act.dma_start(pb2[:, b * C:(b + 1) * C], proj_b.rearrange("(o c) -> o c", o=1)).then_inc(par_loaded, 16)
            act.dma_start(bT[:, :, :], ffn_bT.rearrange("(k p) n -> p k n", p=P)).then_inc(par_loaded, 16)
            act.sem_inc(hT_evac, 2)
            act.sem_inc(d_copied, 2)

            def copy(o, i, scale=1.0):
                return nc.scalar.activation(o, i, ACT.Copy, scale=scale)

            act.wait_ge(wprod_done, 1)
            copy(G[:, 0, :], bk[0][:, 0:C + 1]).then_inc(wprod_evac, 1)
            copy(G[:, 1, :], bk[1][:, 0:C + 1]).then_inc(wprod_evac, 1)
            copy(U, bk[2][:, :].rearrange("p (k c) -> p k c", k=K)).then_inc(wprod_evac, 1)
            copy(g_row, bk[3][0:1, 0:C + 1]).then_inc(wprod_evac, 1)
            copy(u_row, psL[0:1, 1536:1536 + C]).then_inc(wprod_evac, 1)
            for b in range(B):
                act.wait_ge(xh_used, NJ * (b + 1))
                for k in range(K):
                    copy(S_sb[:, b, k, :], psL[:, (b * K + k) * 512:(b * K + k) * 512 + C + 1]).then_inc(S_evac, 1)
            act.wait_ge(crow_done, 1)
            copy(c_row, bk[3][0:1, :]).then_inc(crow_evac, 1)
            act.wait_ge(R_done, 1)
            for b in range(B):
                copy(R[:, b], bk[b][:, :].rearrange("p (k c) -> p k c", k=K)).then_inc(R_evac, 1)
            copy(r_row, bk[2][0:1, :]).then_inc(R_evac, 1)
            act.wait_ge(A_done, 1)
            for b in range(B):
                copy(A_sb[:, b], psL[:, b * 512:(b + 1) * 512].rearrange("p (k c) -> p k c", k=K),
                     scale=1.0 / math.sqrt(C)).then_inc(A_evac, 1)
            act.wait_ge(abc_done, 1)
            copy(abc[:, :, :], psL[:, 1024:1536].rearrange("p (b c) -> p b c", b=B)).then_inc(abc_ready, 1)

            with act.Fori(0, NG) as g:
                for jj in range(GJ):
                    act.wait_ge(hT_done, g * GJ + jj + 3)
                    act.wait_ge(y_done, g * GJ + jj + 1)
                    copy(xT[:, jj % 2, :], bk[jj % 2][:, :]).then_inc(hT_evac, 1)
                act.wait_ge(r2_ready, g + 1)
                for jj in range(GJ):
                    for b in range(B):
                        i = jj * B + b
                        ins = nc.scalar.activation(yb[:, jj, b, :], yb[:, jj, b, :], ACT.Identity,
                                                   bias=nm[:, i:i + 1], scale=rr[:, i:i + 1])
                ins.then_inc(z_ready, 1)
                act.wait_ge(x3_ready, g + 1)
                for b in range(B):
                    copy(x3n[:, b, bass.ds(g * GJ, GJ), 0, :], x3f[:, :, b, :]).then_inc(x3h_ready, 1)
                for jj in range(GJ):
                    act.wait_ge(x3T_done, g * GJ + jj + 1)
                    pv = psL[:, (jj % 2) * 512:(jj % 2 + 1) * 512].rearrange("p (w k t) -> p w k t", w=2, k=K)
                    cols = bass.ds((g * GJ + jj) * P, P)
                    copy(xT1[:, 0, :, cols], pv[:, 0])
                    copy(xdT[:, 0, :, cols], pv[:, 1]).then_inc(x3Th_ready, 1)

            def block_act(nb, with_y):
                for j in range(NJ):
                    act.wait_ge(d_done, nb * NJ + (j + 1))
                    act.wait_ge(s_split, nb * NJ + (j + 1))
                    for s in range(B):
                        ins = nc.scalar.activation(sF[:, j % 2, s, :], bk[j % 2][:, :], ACT.Sigmoid,
                                                   scale=kap[:, s:s + 1])
                    ins.then_inc(s_ready, 1)
                    act.wait_ge(d_stored[j % 2], nb * (8 * NJ) + (16 * (j // 2) + 16))
                    copy(dS[:, j % 2, :], bk[j % 2][:, :]).then_inc(d_copied, 1)
                    if with_y and (j % 4 == 1 and j > 1):
                        y_evac(nb - 1, (j - 5) // 4)
                if with_y:
                    y_evac(nb - 1, 3)

            def y_evac(yb_, q):
                act.wait_ge(yN_done, yb_ * TB + (q + 2))
                copy(yf[:, :, bass.ds(yb_ * TB + q, 1), :].rearrange("p b t c -> p b (t c)"),
                     bk[3][:, :].rearrange("p (b c) -> p b c", b=B)).then_inc(yN_evac, 1)

            act.wait_ge(phi_split, 1)
            block_act(0, False)
            with act.Fori(1, NB) as nb:
                block_act(nb, True)
            for q in range(TB):
                y_evac(NB - 1, q)

            act.wait_ge(gmax_in, 3)
            act.wait_ge(slots_used, NB * NJ + 2)
            act.wait_ge(yN_evac, NB * TB + 1)
            for b in (1, 0):
                for h in range(2):
                    t8 = slice(8 * h, 8 * h + 8)
                    nc.scalar.activation(yhl[:, b, t8, 0, :], yf[:, b, t8, :], ACT.Identity,
                                         scale=sg[:, 1:2]).then_inc(yh_ready, 1)

            def hi(m, gq):
                act.wait_ge(eT_done, m + 1)
                act.wait_ge(comb_done, m + 1)
                copy(eT[:, gq, 0, :], bk[gq % 2][:, :]).then_inc(eTh_ready, 1)

            def expo(b, j, half):
                src, dst = (psL, E1) if b else (l0, E0)
                w = 1 - b
                nc.scalar.activation(dst[:, 1024 * half:1024 * half + 1024], src[:, 1024 * half:1024 * half + 1024],
                                     ACT.Exp, bias=ebias[:, w:w + 1], scale=kap[:, 0:1],
                                     accum_out=zz[:, w, bass.ds(j, 1), half]).then_inc(
                                         E1_ready if b else E0_ready, 1)

            def c1_copy(b, seq, m_end):
                act.wait_ge(comb_done, m_end + 4)
                act.wait_ge(u_ready, seq + 1)
                copy(c1[:, 1 - b, :], bk[3 - b][:, 256:512]).then_inc(c1_ready, 1)

            def comb_act(j, first):
                if not first:
                    hi(8 * j - 4, 0)
                    hi(8 * j - 3, 1)
                    c1_copy(1, 2 * j - 2, 8 * j - 4)
                    hi(8 * j - 2, 2)
                act.wait_ge(m1_ready, j + 1)
                expo(1, j, 0)
                if not first:
                    hi(8 * j - 1, 3)
                expo(1, j, 1)
                hi(8 * j, 0)
                hi(8 * j + 1, 1)
                act.wait_ge(m0_ready, j + 1)
                expo(0, j, 0)
                hi(8 * j + 2, 2)
                expo(0, j, 1)
                if not first:
                    c1_copy(0, 2 * j - 1, 8 * j)
                hi(8 * j + 3, 3)

            comb_act(0, True)
            with act.Fori(1, NJ) as j:
                comb_act(j, False)
            hi(8 * NJ - 4, 0)
            hi(8 * NJ - 3, 1)
            c1_copy(1, 2 * NJ - 2, 8 * NJ - 4)
            hi(8 * NJ - 2, 2)
            hi(8 * NJ - 1, 3)
            c1_copy(0, 2 * NJ - 1, 8 * NJ)

        @block.vector
        def _(dve):
            own = Count(dve, dve_own)
            V = nc.vector
            dve.sem_inc(y_read, 2)
            dve.sem_inc(s_split, 2)
            dve.sem_inc(slots_evac, 4)
            dve.sem_inc(eTl_ready, 2)
            dve.sem_inc(u_ready, 2)
            for i in range(2):
                dve.sem_inc(d_stored[i], 16)
                dve.sem_inc(out_stored[i], 16)

            own.add(V.memset(xbuf[:, :, C:C + 1], 1.0))
            dve.wait_ge(par_loaded, 16 * N_PAR)
            for s in range(KS):
                own.add(V.tensor_tensor_reduce(junk, w_raw[:, s, :], bbc, 1.0, 0.0, ALU.mult, ALU.add, bcol[:, s:s + 1]))
                own.wait()
            own.add(V.tensor_tensor(w_aug[:, :, 0:C], w_raw, wbc.unsqueeze(1).broadcast_to([P, KS, C]), ALU.mult))
            V.tensor_tensor(w_aug[:, :, C], bcol, qbc, ALU.add).then_inc(waug_ready, 1)

            for g in range(4):
                b, h = g // 2, g % 2
                dve.wait_ge(x_loaded[g], 16)
                if g:
                    own.wait()
                for i in range(8):
                    own.add(V.bn_stats(stat[:, i, :], xres[:, b, 8 * h + i, :]))
                own.wait()
                for i in range(7):
                    own.add(V.bn_aggr(mvx[:, b, 8 * h + i, :], stat[:, i, :]))
                V.bn_aggr(mvx[:, b, 8 * h + 7, :], stat[:, 7, :]).then_inc(stats_x, 1)
                dve.wait_ge(rstd_x, g + 1)
                own.wait()
                for i in range(8):
                    t = 8 * g + i
                    if t >= 4:
                        dve.wait_ge(xh_used, t - 3)
                    j = 8 * h + i
                    V.tensor_scalar(xbuf[:, t % 4, 0:C], xres[:, b, j, :], mvx[:, b, j, 0:1], rx[:, 1, b, j:j + 1],
                                    ALU.subtract, ALU.mult).then_inc(xh_ready, 1)

            def pow2_scale(i):
                c = slice(i, i + 1)
                own.add(V.tensor_scalar(gm[:, c], gm[:, c], 2.0 ** -100, None, ALU.max))
                own.wait()
                own.add(V.tensor_scalar(gm[:, c].bitcast(I32), gm[:, c].bitcast(I32), 0x7F800000, None, ALU.bitwise_and))
                own.wait()
                own.add(V.tensor_scalar(isg[:, c], gm[:, c], 2.0 ** -TOP_EXP, None, ALU.mult))
                own.wait()
                own.add(V.reciprocal(sg[:, c], isg[:, c]))
                own.wait()

            dve.wait_ge(phi_loaded, 16)
            V.tensor_reduce(pm[:, 0:1], phf.rearrange("p k n -> p (k n)"), AX_X, ALU.max,
                            apply_absolute_value=True).then_inc(gmax_in, 1)
            dve.wait_ge(gmax_out, 1)
            pow2_scale(0)
            own.add(V.tensor_scalar(kap[:, 0:1], isg[:, 0:1], 1.0 / X_SCALE, None, ALU.mult))
            own.add(V.tensor_scalar(kap[:, 1:2], isg[:, 0:1], -1.0 / X_SCALE, None, ALU.mult))
            own.add(V.tensor_scalar(phs[:, 0], phf, sg[:, 0:1], None, ALU.mult))
            own.wait()
            V.scalar_tensor_tensor(phs[:, 1].rearrange("p k n -> p (k n)"), phf.rearrange("p k n -> p (k n)"),
                                   sg[:, 0:1], phs[:, 0].rearrange("p k n -> p (k n)"), ALU.mult,
                                   ALU.subtract).then_inc(phi_split, 1)

            dve.wait_ge(A_done, 1)
            V.scalar_tensor_tensor(a_row, bk[3][0:1, :], 1.0 / math.sqrt(C), pb2, ALU.mult, ALU.add).then_inc(arow_ready, 1)

            dve.wait_ge(xh_used, B * NJ)
            with dve.Fori(0, NG) as g:
                own.enter(g, 27)
                t0 = g * GJ

                def xhat(jj):
                    dve.wait_ge(hT_done, t0 + jj + 1)
                    for b in range(B):
                        ins = V.tensor_scalar(xbuf[:, 2 * (jj % 2) + b, 0:C],
                                              xres[:, b, bass.ds(t0 + jj, 1), :].rearrange("p j c -> p (j c)"),
                                              mvx[:, b, bass.ds(t0 + jj, 1), 0], rx[:, 1, b, bass.ds(t0 + jj, 1)],
                                              ALU.subtract, ALU.mult)
                    ins.then_inc(xh_ready, 1)

                def attn(jj):
                    dve.wait_ge(y_done, t0 + jj + 3)
                    V.tensor_tensor(yb[:, jj], bk[2 + jj % 2][:, :].rearrange("p (b c) -> p b c", b=B),
                                    x1a[:, jj], ALU.add).then_inc(y_read, 1)

                xhat(0)
                xhat(1)
                dve.wait_ge(x1a_ready, 2 * g + 2)
                xhat(2)
                attn(0)
                xhat(3)
                for jj in range(1, GJ):
                    attn(jj)
                dve.wait_ge(y_read, t0 + GJ + 2)
                for i in range(8):
                    own.add(V.bn_stats(stat[:, i, :], yb[:, i // 2, i % 2, :]))
                own.wait_apart()
                for i in range(8):
                    ins = V.bn_aggr(mv[:, i, :], stat[:, i, :])
                ins.then_inc(mv_ready, 1)
                dve.wait_ge(mv_ready, 2 * g + 1)
                wait_apart(dve, x2_ready, 2 * g + 2)
                for i in range(8):
                    own.add(V.bn_stats(stat[:, i, :], xres[:, i % 2, bass.ds(t0 + i // 2, 1), :].rearrange("p j c -> p (j c)")))
                own.wait_apart()
                for i in range(8):
                    ins = V.bn_aggr(mv[:, i, :], stat[:, i, :])
                ins.then_inc(mv_ready, 1)
                dve.wait_ge(mv_ready, 2 * g + 2)
                dve.wait_ge(r3_ready, g + 1)
                for i in range(8):
                    ins = V.tensor_scalar(x3f[:, i // 2, i % 2, :],
                                          xres[:, i % 2, bass.ds(t0 + i // 2, 1), :].rearrange("p j c -> p (j c)"),
                                          mv[:, i, 0:1], rr[:, i:i + 1], ALU.subtract, ALU.mult)
                    if i < 7:
                        own.add(ins)
                ins.then_inc(x3_ready, 1)
                own.wait()
                dve.wait_ge(x3_ready, g + 1)
                for b in range(B):
                    dve.wait_ge(x3h_ready, 2 * g + b + 1)
                    V.tensor_tensor(x3n[:, b, bass.ds(t0, GJ), 1, :], x3f[:, :, b, :],
                                    x3n[:, b, bass.ds(t0, GJ), 0, :], ALU.subtract).then_inc(x3l_ready, 1)
                for jj in range(GJ):
                    dve.wait_ge(x3Th_ready, t0 + jj + 1)
                    pv = psL[:, (jj % 2) * 512:(jj % 2 + 1) * 512].rearrange("p (w k t) -> p w k t", w=2, k=K)
                    cols = bass.ds((t0 + jj) * P, P)
                    own.add(V.tensor_tensor(xT1[:, 1, :, cols], pv[:, 0], xT1[:, 0, :, cols], ALU.subtract))
                    V.tensor_tensor(xdT[:, 1, :, cols], pv[:, 1], xdT[:, 0, :, cols], ALU.subtract).then_inc(x3Tl_ready, 1)
                own.leave(NG)

            def block_dve(nb, with_y):
                for j in range(NJ):
                    dve.wait_ge(s_ready, nb * NJ + (j + 1))
                    dve.wait_ge(slots_used, nb * NJ + (j + 1))
                    own.add(V.tensor_scalar(shl[:, j % 2, 0], sF[:, j % 2], S_SCALE, None, ALU.mult))
                    own.wait()
                    V.scalar_tensor_tensor(shl[:, j % 2, 1], sF[:, j % 2], S_SCALE, shl[:, j % 2, 0],
                                           ALU.mult, ALU.subtract).then_inc(s_split, 1)
                    if with_y and j % 4 == 2:
                        y_bias(nb - 1, j // 4)
                dve.wait_ge(slots_used, nb * NJ + (NJ + 2))
                slots_out(nb)

            def slots_out(nb):
                for k in range(K):
                    for b in range(B):
                        i = k * B + b
                        V.tensor_scalar(slT[:, k, :, b, :],
                                        psL[:, i * 512:(i + 1) * 512].rearrange("p (n q) -> p n q", q=Q),
                                        1.0 / (X_SCALE * S_SCALE), None, ALU.mult).then_inc(slots_evac, 1)

            def y_bias(yb_, q):
                dve.wait_ge(yTp_done, yb_ * TB + (q + 1))
                dve.wait_ge(yN_done, yb_ * TB + (q + 1))
                own.wait()
                for e in range(K):
                    V.tensor_tensor(
                        yT[:, e].rearrange("p b (n q) -> p b n q", q=Q),
                        bk[2][:, e * 256:(e + 1) * 256].rearrange("p (n b q) -> p b n q", n=EP, b=B),
                        bT[:, e, bass.ds((yb_ * TB + q) * EP, EP)].unsqueeze(1).unsqueeze(3).broadcast_to([P, B, EP, Q]),
                        ALU.add).then_inc(yT_ready, 1)
                dve.wait_ge(yT_ready, (yb_ * TB + q) * 2 + 4)
                own.add(V.tensor_reduce(ymx[:, bass.ds(yb_ * TB + q, 1)], yT.rearrange("p e b n -> p (e b n)"),
                                        AX_X, ALU.max, apply_absolute_value=True))

            own.enter(0, NJ)
            block_dve(0, False)
            own.leave(1)
            with dve.Fori(1, NB) as nb:
                own.enter(nb - 1, NJ + TB)
                block_dve(nb, True)
                own.leave(NB - 1)
            for q in range(TB):
                y_bias(NB - 1, q)
            own.wait()
            V.tensor_reduce(pm[:, 1:2], ymx, AX_X, ALU.max).then_inc(gmax_in, 1)
            dve.wait_ge(gmax_out, 2)
            pow2_scale(1)
            dve.sem_inc(gmax_in, 1)

            def lo(m, gq):
                dve.wait_ge(eTh_ready, m + 1)
                V.tensor_tensor(eT[:, gq, 1, :], bk[gq % 2][:, :], eT[:, gq, 0, :], ALU.subtract).then_inc(eTl_ready, 1)

            def maxima(j, w, last):
                own.wait()
                own.add(V.tensor_reduce(m1[:, w:w + 1], m4[:, 4 * w:4 * w + 4], AX_X, ALU.max))
                own.wait()
                V.tensor_scalar(ebias[:, w:w + 1], m1[:, w:w + 1], kap[:, 1:2], E_LOG, ALU.mult, ALU.add).then_inc(last, 1)

            def add_max(j, kb):
                c = slice(512 * kb, 512 * kb + 512)
                own.add(V.tensor_tensor_reduce(l0[:, c], psL[:, c], dB[:, c], 1.0, -3.0e38, ALU.add, ALU.max,
                                               m4[:, 4 + kb:5 + kb]))

            def tail(b, seq):
                w = 1 - b
                dve.wait_ge(c1_ready, seq + 1)
                own.add(V.tensor_tensor(u[:, w, :], bk[3 - b][:, 0:256], c1[:, w, :], ALU.add))
                own.wait()
                own.add(V.bn_stats(stat[:, w, :], u[:, w, :]))
                own.wait_apart()
                V.bn_aggr(mvC[:, w, :], stat[:, w, :]).then_inc(u_ready, 1)

            def comb_dve(j, first):
                if not first:
                    lo(8 * j - 4, 0)
                    lo(8 * j - 3, 1)
                    dve.wait_ge(fin_ready, 2 * j - 1)
                    tail(1, 2 * j - 2)
                for kb in range(4):
                    dve.wait_ge(l_done, 4 * j + kb + 1)
                    own.add(V.tensor_reduce(m4[:, kb:kb + 1], psL[:, 512 * kb:512 * kb + 512], AX_X, ALU.max))
                maxima(j, 0, m1_ready)
                if not first:
                    lo(8 * j - 2, 2)
                    dve.wait_ge(E0_ready, 2 * j)
                dve.wait_ge(dB_loaded, 16 * j + 16)
                wait_apart(dve, E1_ready, 2 * j + 1)
                add_max(j, 0)
                add_max(j, 1)
                if not first:
                    lo(8 * j - 1, 3)
                wait_apart(dve, E1_ready, 2 * j + 2)
                add_max(j, 2)
                add_max(j, 3)
                maxima(j, 1, m0_ready)
                for gq in range(3):
                    lo(8 * j + gq, gq)
                if not first:
                    dve.wait_ge(fin_ready, 2 * j)
                    tail(0, 2 * j - 1)
                lo(8 * j + 3, 3)

            def y_lo():
                for i, (b, h) in enumerate(((1, 0), (1, 1), (0, 0), (0, 1))):
                    t8 = slice(8 * h, 8 * h + 8)
                    dve.wait_ge(yh_ready, i + 1)
                    V.scalar_tensor_tensor(yhl[:, b, t8, 1, :], yf[:, b, t8, :], sg[:, 1:2], yhl[:, b, t8, 0, :],
                                           ALU.mult, ALU.subtract).then_inc(yl_ready, 1)

            y_lo()
            own.enter(0, 10)
            comb_dve(0, True)
            own.leave(1)
            with dve.Fori(1, NJ) as j:
                own.enter(j - 1, 10 + 4)
                comb_dve(j, False)
                own.leave(NJ - 1)
            lo(8 * NJ - 4, 0)
            lo(8 * NJ - 3, 1)
            dve.wait_ge(fin_ready, 2 * NJ - 1)
            tail(1, 2 * NJ - 2)
            lo(8 * NJ - 2, 2)
            lo(8 * NJ - 1, 3)
            dve.wait_ge(fin_ready, 2 * NJ)
            tail(0, 2 * NJ - 1)

        @block.tensor
        def _(pe):
            mm = nc.tensor.matmul
            pe.sem_inc(hT_done, 2)
            pe.sem_inc(y_done, 2)
            pe.sem_inc(slots_used, 2)
            pe.sem_inc(comb_done, 4)

            pe.wait_ge(waug_ready, 1)
            wq, wk, wv = w_aug[:, 0:K], w_aug[:, K:2 * K], w_aug[:, 2 * K:3 * K]
            for i in range(K):
                for k in range(K):
                    mm(bk[i][:, 0:C + 1], wk[:, k, i * P:(i + 1) * P], wq[:, k, :], start=(k == 0), stop=(k == K - 1))
            for i in range(K):
                for k in range(K):
                    mm(bk[2][:, i * C:(i + 1) * C], wv[:, k, i * P:(i + 1) * P], wpT[:, k, :], start=(k == 0), stop=(k == K - 1))
            for k in range(K):
                mm(bk[3][0:1, 0:C + 1], wk[:, k, C:C + 1], wq[:, k, :], start=(k == 0), stop=(k == K - 1))
            for k in range(K):
                ins = mm(psL[0:1, 1536:1536 + C], wv[:, k, C:C + 1], wpT[:, k, :], start=(k == 0), stop=(k == K - 1))
            ins.then_inc(wprod_done, 1)

            for b in range(B):
                if b == 1:
                    pe.wait_ge(wprod_evac, 5)
                for j in range(NJ):
                    t = b * NJ + j
                    pe.wait_ge(xh_ready, t + 1)
                    for k in range(K):
                        o = (b * K + k) * 512
                        ins = mm(psL[:, o:o + C + 1], xbuf[:, t % 4, k * P:(k + 1) * P], xbuf[:, t % 4, :],
                                 start=(j == 0), stop=(j == NJ - 1))
                    ins.then_inc(xh_used, 1)

            pe.wait_ge(pool_const, 1)
            pe.wait_ge(S_evac, 4)
            for b in range(B):
                for k in range(K):
                    ins = mm(bk[3][0:1, b * C + k * P:b * C + (k + 1) * P], S_sb[:, b, k, C:C + 1], ident[:, :],
                             start=True, stop=True)
            ins.then_inc(crow_done, 1)
            for b in range(B):
                for i in range(K):
                    for k in range(K):
                        mm(bk[b][:, i * C:(i + 1) * C], S_sb[:, b, k, i * P:(i + 1) * P], U[:, k, :], start=(k == 0), stop=False)
                    if b == 0 and i == 0:
                        pe.wait_ge(crow_evac, 1)
                    mm(bk[b][:, i * C:(i + 1) * C], c_row[:, b * C + i * P:b * C + (i + 1) * P], u_row, start=False, stop=True)
            for b in range(B):
                for k in range(K):
                    mm(bk[2][0:1, b * C:(b + 1) * C], S_sb[:, b, k, C:C + 1], U[:, k, :], start=(k == 0), stop=False)
                ins = mm(bk[2][0:1, b * C:(b + 1) * C], tcount[:, :], u_row, start=False, stop=True)
            ins.then_inc(R_done, 1)
            pe.wait_ge(R_evac, 3)
            for b in range(B):
                for i in range(K):
                    for k in range(K):
                        mm(psL[:, b * 512 + i * C:b * 512 + (i + 1) * C], G[:, k, i * P:(i + 1) * P], R[:, b, k, :], start=(k == 0), stop=False)
                    mm(psL[:, b * 512 + i * C:b * 512 + (i + 1) * C], g_row[:, i * P:(i + 1) * P], r_row[:, b * C:(b + 1) * C], start=False, stop=True)
            for b in range(B):
                for k in range(K):
                    mm(bk[3][0:1, b * C:(b + 1) * C], G[:, k, C:C + 1], R[:, b, k, :], start=(k == 0), stop=False)
                ins = mm(bk[3][0:1, b * C:(b + 1) * C], g_row[:, C:C + 1], r_row[:, b * C:(b + 1) * C], start=False, stop=True)
            ins.then_inc(A_done, 1)
            pe.wait_ge(arow_ready, 1)
            mm(psL[:, 1024:1536], ones[:, :], a_row, start=True, stop=True).then_inc(abc_done, 1)
            pe.wait_ge(A_evac, 2)
            pe.wait_ge(abc_ready, 1)

            with pe.Fori(0, NG) as g:
                t0 = g * GJ

                def h_transpose(jj):
                    pe.wait_ge(xh_ready, t0 + jj + (B * NJ + 1))
                    pe.wait_ge(hT_evac, t0 + jj + 1)
                    for b in range(B):
                        for k in range(K):
                            i = b * K + k
                            ins = nc.tensor.transpose(bk[jj % 2][:, i * P:(i + 1) * P],
                                                      xbuf[:, 2 * (jj % 2) + b, k * P:(k + 1) * P], ident[:, :])
                    ins.then_inc(hT_done, 1)

                def h_product(jj):
                    pe.wait_ge(hT_evac, t0 + jj + 3)
                    pe.wait_ge(y_read, t0 + jj + 1)
                    for b in range(B):
                        for k in range(K):
                            i = b * K + k
                            ins = mm(bk[2 + jj % 2][:, b * C:(b + 1) * C], xT[:, jj % 2, i * P:(i + 1) * P],
                                     A_sb[:, b, k, :], start=(k == 0), stop=(k == K - 1))
                    ins.then_inc(y_done, 1)

                h_transpose(0)
                h_transpose(1)
                for jj in range(GJ):
                    h_product(jj)
                    if jj + 2 < GJ:
                        h_transpose(jj + 2)
                pe.wait_ge(x3_ready, g + 1)
                pe.wait_ge(xd_ready, g + 1)
                for jj in range(GJ):
                    if jj >= 2:
                        pe.wait_ge(x3Tl_ready, t0 + jj - 1)
                    for w in range(2):
                        for k in range(K):
                            src = xd[:, jj, k * P:(k + 1) * P] if w else x3f[:, jj, 1, k * P:(k + 1) * P]
                            o = (jj % 2) * 512 + (w * K + k) * P
                            ins = nc.tensor.transpose(psL[:, o:o + P], src, ident[:, :])
                    ins.then_inc(x3T_done, 1)
                pe.wait_ge(x3Tl_ready, t0 + GJ)

            pe.wait_ge(phi_split, 1)
            pe.wait_ge(x3l_ready, 2 * NG)

            def d_tile(nb, j):
                pe.wait_ge(d_copied, nb * NJ + (j + 1))
                for k in range(K):
                    for hx, hp in ((0, 0), (0, 1), (1, 0)):
                        ins = mm(bk[j % 2][:, :], xdT[:, hx, k, j * P:(j + 1) * P], phs[:, hp, k, bass.ds(nb * 512, 512)],
                                 start=(k == 0 and hx + hp == 0), stop=(k == K - 1 and hx == 1))
                ins.then_inc(d_done, 1)

            def slots(nb, j):
                pe.wait_ge(s_split, nb * NJ + (j + 3))
                if j == 0:
                    pe.wait_ge(slots_evac, nb * 4 + 4)
                for k in range(K):
                    for b in range(B):
                        i = k * B + b
                        for hx, hs in ((0, 0), (0, 1), (1, 0)):
                            ins = mm(psL[:, i * 512:(i + 1) * 512], x3n[:, b, j, hx, k * P:(k + 1) * P],
                                     shl[:, j % 2, hs, b, :], start=(j == 0 and hx + hs == 0), stop=(j == NJ - 1 and hx == 1))
                ins.then_inc(slots_used, 1)

            def y_product(yb_, q):
                pe.wait_ge(W_loaded[q % 2], yb_ * (8 * TB) + (16 * (q // 2) + 16))
                if q == 0:
                    pe.wait_ge(slots_evac, yb_ * 4 + 8)
                pe.wait_ge(yT_ready, (yb_ * TB + q) * 2 + YT0)
                for n in range(EP):
                    for e in range(K):
                        for k in range(K):
                            o = e * 256 + n * 64
                            ins = mm(bk[2][:, o:o + 64], Wt[:, q % 2, n, k, e * P:(e + 1) * P],
                                     slT[:, k, q * EP + n].rearrange("p b q -> p (b q)"), start=(k == 0), stop=(k == K - 1))
                ins.then_inc(yTp_done, 1)

            def y_turn(yb_, q):
                pe.wait_ge(yT_ready, (yb_ * TB + q) * 2 + YT0 + 2)
                pe.wait_ge(yN_evac, yb_ * TB + q + 1)
                for b in range(B):
                    for e in range(K):
                        o = b * 256 + e * P
                        ins = nc.tensor.transpose(bk[3][:, o:o + P], yT[:, e, b, :], ident[:, :])
                ins.then_inc(yN_done, 1)

            YT0 = 2
            pe.sem_inc(yT_ready, 2)
            pe.sem_inc(yN_evac, 1)
            pe.sem_inc(yN_done, 1)

            def block_pe(nb, with_y):
                d_tile(nb, 0)
                d_tile(nb, 1)
                for j in range(NJ):
                    slots(nb, j)
                    if with_y and j % 4 == 1:
                        y_product(nb - 1, j // 4)
                    if j + 2 < NJ:
                        d_tile(nb, j + 2)
                    if with_y and j % 4 == 3:
                        y_turn(nb - 1, j // 4)

            block_pe(0, False)
            with pe.Fori(1, NB) as nb:
                block_pe(nb, True)

            def logits(j, kbs):
                for kb in kbs:
                    for k in range(K):
                        for hx, hp in ((0, 0), (0, 1), (1, 0)):
                            ins = mm(psL[:, kb * 512:(kb + 1) * 512], xT1[:, hx, k, bass.ds(j * P, P)],
                                     phs[:, hp, k, kb * 512:(kb + 1) * 512],
                                     start=(k == 0 and hx + hp == 0), stop=(k == K - 1 and hx == 1))
                    ins.then_inc(l_done, 1)

            def turn(b, j, m, gq):
                pe.wait_ge(E1_ready if b else E0_ready, 2 * j + 1 + gq // 2)
                pe.wait_ge(eTl_ready, m + 1)
                E = E1 if b else E0
                for i in range(4):
                    o = gq * 512 + i * P
                    ins = nc.tensor.transpose(bk[gq % 2][:, i * P:(i + 1) * P], E[:, o:o + P], ident[:, :])
                ins.then_inc(eT_done, 1)

            def high(b, seq, m, gq):
                pe.wait_ge(eTh_ready, m + 1)
                if gq == 0:
                    pe.wait_ge(u_ready, seq + 1)
                for i in range(4):
                    t = gq * 4 + i
                    mm(bk[3 - b][:, :], eT[:, gq, 0, i * P:(i + 1) * P], yhl[:, b, t].rearrange("p h c -> p (h c)"),
                       start=(t == 0), stop=False)

            def low(b, m, gq):
                pe.wait_ge(eTl_ready, m + 3)
                for i in range(4):
                    t = gq * 4 + i
                    ins = mm(bk[3 - b][:, 256:512], eT[:, gq, 1, i * P:(i + 1) * P], yhl[:, b, t, 0, :],
                             start=False, stop=(t == NT - 1))
                ins.then_inc(comb_done, 1)

            def comb_pe(j, first):
                m = 8 * j
                if first:
                    turn(1, j, m, 0)
                    turn(1, j, m + 1, 1)
                else:
                    turn(0, j - 1, m - 3, 1)
                    low(1, m - 5, 3)
                    logits(j, range(4))
                    pe.wait_ge(yl_ready, 4)
                    high(0, 2 * j - 1, m - 4, 0)
                    turn(0, j - 1, m - 2, 2)
                    high(0, 2 * j - 1, m - 3, 1)
                    turn(0, j - 1, m - 1, 3)
                    low(0, m - 4, 0)
                    high(0, 2 * j - 1, m - 2, 2)
                    turn(1, j, m, 0)
                    low(0, m - 3, 1)
                    high(0, 2 * j - 1, m - 1, 3)
                    turn(1, j, m + 1, 1)
                    low(0, m - 2, 2)
                if first:
                    pe.wait_ge(yl_ready, 1)
                high(1, 2 * j, m, 0)
                turn(1, j, m + 2, 2)
                if not first:
                    low(0, m - 1, 3)
                high(1, 2 * j, m + 1, 1)
                turn(1, j, m + 3, 3)
                low(1, m, 0)
                if first:
                    pe.wait_ge(yl_ready, 2)
                high(1, 2 * j, m + 2, 2)
                turn(0, j, m + 4, 0)
                low(1, m + 1, 1)
                high(1, 2 * j, m + 3, 3)
                low(1, m + 2, 2)

            for q in range(TB):
                y_product(NB - 1, q)
                logits(0, (q,))
                y_turn(NB - 1, q)
            comb_pe(0, True)
            with pe.Fori(1, NJ) as j:
                comb_pe(j, False)
            m = 8 * NJ
            turn(0, NJ - 1, m - 3, 1)
            low(1, m - 5, 3)
            high(0, 2 * NJ - 1, m - 4, 0)
            turn(0, NJ - 1, m - 2, 2)
            high(0, 2 * NJ - 1, m - 3, 1)
            turn(0, NJ - 1, m - 1, 3)
            low(0, m - 4, 0)
            high(0, 2 * NJ - 1, m - 2, 2)
            low(0, m - 3, 1)
            high(0, 2 * NJ - 1, m - 1, 3)
            low(0, m - 2, 2)
            low(0, m - 1, 3)


def kernel(**inputs):
    import numpy as np
    import concourse.bacc as bacc
    from concourse.bass_utils import run_bass_kernel_spmd

    nc = bacc.Bacc("TRN2", target_bir_lowering=False, num_devices=1)
    laid = {
        "x": inputs["L0_attn_x"],
        "norm_w": inputs["L0_attn_norm_w"],
        "norm_b": inputs["L0_attn_norm_b"],
        "qkv_w": inputs["L0_attn_qkv_w"],
        "qkv_b": np.reshape(inputs["L0_attn_qkv_b"], (-1, 128)).T,
        "proj_wT": np.transpose(inputs["L0_attn_proj_w"]),
        "proj_b": inputs["L0_attn_proj_b"],
        "phi": inputs["L0_ffn_phi"],
        "ffn_w": inputs["L0_ffn_W"],
        "ffn_bT": np.transpose(inputs["L0_ffn_b"]),
    }
    arrays, args = {}, []
    for name, a in laid.items():
        a = np.ascontiguousarray(a)
        arrays[f"in_{name}"] = a
        args.append(nc.dram_tensor(f"in_{name}", a.shape, mybir.dt.from_np(a.dtype), kind="ExternalInput").ap())
    out = nc.dram_tensor("out", laid["x"].shape, F32, kind="ExternalOutput").ap()
    build(nc, *args, out)
    r = run_bass_kernel_spmd(nc, [arrays], core_ids=[0])
    return r.results[0]["out"]
```

```python
import math
from contextlib import ExitStack

import concourse.bass as bass
from concourse import mybir

F32 = mybir.dt.float32
F16 = mybir.dt.float16
I32 = mybir.dt.int32
ALU = mybir.AluOpType
ACT = mybir.ActivationFunctionType
AX_X = mybir.AxisListType.X

P = 128
EPS = 1e-5
X_SCALE = 2.0 ** 10
S_SCALE = 2.0 ** 12
E_LOG = 14 * math.log(2.0)
TOP_EXP = 13


class Arena:

    def __init__(self, tensor, words):
        self.tensor, self.words, self.at = tensor, words, 0

    def take(self, words, dtype=F32, rows=P):
        assert self.at + words <= self.words, (self.at, words, self.words)
        view = self.tensor[0:rows, self.at:self.at + words]
        self.at += words
        return view if dtype == F32 else view.bitcast(dtype)


PASSED = []


def wait_apart(eng, sem, value):
    eng.wait_ge(sem, value)
    eng.sem_inc(PASSED[0], 1)


class Count:

    def __init__(self, eng, sem):
        self.eng, self.sem, self.base, self.n = eng, sem, 0, 0

    def add(self, ins):
        ins.then_inc(self.sem, 1)
        self.n += 1
        return ins

    def wait(self):
        self.eng.wait_ge(self.sem, self.base + self.n)

    def wait_apart(self):
        wait_apart(self.eng, self.sem, self.base + self.n)

    def enter(self, i, per):
        self.outer = (self.base, self.n, per)
        self.base, self.n = self.base + self.n + i * per, 0

    def leave(self, turns):
        base, n, per = self.outer
        assert self.n == per, (self.n, per)
        self.base, self.n = base + n + turns * per, 0


def build(nc, x, norm_w, norm_b, qkv_w, qkv_b, proj_wT, proj_b, phi, ffn_w, ffn_bT, out):
    B, T, C = x.shape
    N, D, _ = ffn_w.shape
    NP = phi.shape[1] * phi.shape[2]
    Q = phi.shape[2]
    NJ = T // P
    K = C // P
    KS = 3 * K
    NB = NP // 512
    NT = NP // P
    TB = 512 // P
    EP = P // Q
    GJ = 4
    NG = NJ // GJ
    assert (B, K, TB) == (2, 2, 4)

    x_v = x.rearrange("b (p j) c -> p b j c", j=NJ)
    out_v = out.rearrange("b (p j) c -> p b j c", j=NJ)
    phi_v = phi.rearrange("(k p) n q -> p k (n q)", p=P)
    w_v = ffn_w.rearrange("(t n) (k p) e -> t p n k e", n=EP, p=P)
    d_dram = nc.dram_tensor("logit_difference", [NJ, P, NP], F32, kind="Internal").ap()

    with ExitStack() as ctx:
        def sb(name, shape, dt=F32):
            return ctx.enter_context(nc.sbuf_tensor(name, shape, dt))

        def sem(name):
            return ctx.enter_context(nc.semaphore(name))

        xres = sb("xres", [P, B, NJ, C])
        phs = sb("phs", [P, 2, K, NP], F16)
        xT1 = sb("xT1", [P, 2, K, T], F16)
        ident = sb("ident", [P, P])
        ones = sb("ones", [1, P])
        tcount = sb("tcount", [1, 1])
        epst = sb("epst", [P, 4])
        A_sb = sb("A_sb", [P, B, K, C])
        abc = sb("abc", [P, B, C])
        bT = sb("bT", [P, K, N])
        stat = sb("stat", [P, 2, 8, 6])
        small = sb("small", [P, 480])
        r_xdT = sb("r_xdT", [P, K * T])
        r_xn = sb("r_xn", [P, B * NJ * C])
        r_y = sb("r_y", [P, B * NT * C])
        r_1 = sb("r_1", [P, 6144])
        r_2 = sb("r_2", [P, 4096 + 2048 + 512])

        xdT = r_xdT[:, :].bitcast(F16).rearrange("p (h k t) -> p h k t", h=2, k=K)
        x3n = r_xn[:, :].bitcast(F16).rearrange("p (b j h c) -> p b j h c", b=B, j=NJ, h=2)
        yhl = r_xn[:, :].bitcast(F16).rearrange("p (b t h c) -> p b t h c", b=B, t=NT, h=2)
        yf = r_y[:, :].rearrange("p (b t c) -> p b t c", b=B, t=NT)

        a = Arena(r_xn, B * NJ * C)
        w_raw = a.take(KS * C).rearrange("p (s c) -> p s c", s=KS)
        w_aug = a.take(KS * (C + 1)).rearrange("p (s c) -> p s c", s=KS)
        wbc = a.take(C)
        bbc = a.take(C)
        junk = a.take(C)
        wpT = a.take(K * C).rearrange("p (k c) -> p k c", k=K)
        G = a.take(K * (C + 1)).rearrange("p (k c) -> p k c", k=K)
        g_row = a.take(C + 1, rows=1)
        u_row = a.take(C, rows=1)
        r_row = a.take(B * C, rows=1)
        c_row = a.take(B * C, rows=1)
        a_row = a.take(B * C, rows=1)
        pb2 = a.take(B * C, rows=1)
        a = Arena(r_y, B * NT * C)
        x1a = a.take(2 * GJ * B * C).rearrange("p (w j b c) -> p w j b c", w=2, j=GJ, b=B)
        at = a.at
        yb = a.take(GJ * B * C).rearrange("p (j b c) -> p j b c", j=GJ, b=B)
        x3f = a.take(GJ * B * C).rearrange("p (j b c) -> p j b c", j=GJ, b=B)
        a.at = at
        U = a.take(K * C).rearrange("p (k c) -> p k c", k=K)
        S_sb = a.take(B * K * (C + 1)).rearrange("p (b k c) -> p b k c", b=B, k=K)
        R = a.take(B * K * C).rearrange("p (b k c) -> p b k c", b=B, k=K)
        a = Arena(r_1, 6144)
        phf = a.take(K * NP).rearrange("p (k n) -> p k n", k=K)
        a = Arena(r_2, 6656)
        Wt = a.take(4096).rearrange("p (w n k e) -> p w n k e", w=2, n=EP, k=K)
        xT = a.take(1024).rearrange("p (w c) -> p w c", w=2)
        xd = a.take(GJ * C).rearrange("p (j c) -> p j c", j=GJ)
        xbuf = sb("xbuf", [P, 4, C + 1])
        a = Arena(r_1, 6144)
        sF = a.take(2048).rearrange("p (w s n) -> p w s n", w=2, s=B)
        shl = a.take(2048, F16).rearrange("p (w h s n) -> p w h s n", w=2, h=2, s=B)
        dS = a.take(1024).rearrange("p (w n) -> p w n", w=2)
        a = Arena(r_2, 6656)
        a.take(4096)
        slT = a.take(2048).rearrange("p (k n b q) -> p k n b q", k=K, n=TB * EP, b=B)
        yT = a.take(512).rearrange("p (e b n) -> p e b n", e=K, b=B)
        a = Arena(r_1, 6144)
        E1, E0, l0 = a.take(2048), a.take(2048), a.take(2048)
        dB = r_xdT[:, 0:2048]
        a = Arena(r_2, 6656)
        eT = a.take(2048, F16).rearrange("p (w h m) -> p w h m", w=4, h=2)
        a = Arena(r_y, B * NT * C)
        c1 = a.take(512).rearrange("p (w c) -> p w c", w=2)
        u = a.take(512).rearrange("p (w c) -> p w c", w=2)
        fo = a.take(512).rearrange("p (w c) -> p w c", w=2)
        fz = a.take(512).rearrange("p (w c) -> p w c", w=2)

        sm = Arena(small, 480)
        bcol, qbc = sm.take(KS), sm.take(KS)
        mvx = sm.take(64).rearrange("p (b j s) -> p b j s", b=B, j=NJ)
        rx = sm.take(96).rearrange("p (s b j) -> p s b j", s=3, b=B)
        mvy = sm.take(16).rearrange("p (i s) -> p i s", s=2)
        mv2 = sm.take(16).rearrange("p (i s) -> p i s", s=2)
        ve = sm.take(16)
        ry = sm.take(8)
        ny = sm.take(2 * NJ)
        r3, n3 = sm.take(8), sm.take(8)
        pm = sm.take(2)
        gm = sm.take(2)
        sg = sm.take(2)
        isg = sm.take(2)
        kap = sm.take(2)
        ymx = sm.take(NT)
        m4 = sm.take(8)
        m1 = sm.take(2)
        ebias = sm.take(2)
        zz = sm.take(4 * NJ).rearrange("p (w j s) -> p w j s", w=2, j=NJ)
        mvC = sm.take(4).rearrange("p (w s) -> p w s", w=2)
        tl = sm.take(16).rearrange("p (w s) -> p w s", w=2)

        psL = ctx.enter_context(nc.psum_tensor("psL", [P, 2048], F32))
        bk = [ctx.enter_context(nc.psum_tensor(f"bk{i}", [P, 512], F32)) for i in range(4)]

        par_loaded = sem("par_loaded")
        x_loaded = [sem(f"x_loaded{g}") for g in range(4)]
        phi_loaded = sem("phi_loaded")
        W_loaded = [sem(f"W_loaded{i}") for i in range(2)]
        pool_const = sem("pool_const")
        PASSED[:] = [sem("passed")]
        dve_own, pool_own = sem("dve_own"), sem("pool_own")
        waug_ready = sem("waug_ready")
        wprod_done, wprod_evac = sem("wprod_done"), sem("wprod_evac")
        stats_x, rstd_x = sem("stats_x"), sem("rstd_x")
        xh_ready, xh_used = sem("xh_ready"), sem("xh_used")
        S_evac = sem("S_evac")
        crow_done, crow_evac = sem("crow_done"), sem("crow_evac")
        R_done, R_evac = sem("R_done"), sem("R_evac")
        A_done, A_evac = sem("A_done"), sem("A_evac")
        arow_ready, abc_done, abc_ready = sem("arow_ready"), sem("abc_done"), sem("abc_ready")
        gmax_in, gmax_out = sem("gmax_in"), sem("gmax_out")
        phi_split = sem("phi_split")
        hT_done, hT_evac = sem("hT_done"), sem("hT_evac")
        y_done, y_read = sem("y_done"), sem("y_read")
        nx_ready, x1_ready, x1a_ready = sem("nx_ready"), sem("x1_ready"), sem("x1a_ready")
        mvy_ready, ry_ready, mv2_ready = sem("mvy_ready"), sem("ry_ready"), sem("mv2_ready")
        r3_ready, x3_ready, x3h_ready, x3l_ready = sem("r3_ready"), sem("x3_ready"), sem("x3h_ready"), sem("x3l_ready")
        xd_ready, x3T_done, x3Th_ready, x3Tl_ready = sem("xd_ready"), sem("x3T_done"), sem("x3Th_ready"), sem("x3Tl_ready")
        d_done, s_ready, d_copied, s_split, slots_used = (
            sem("d_done"), sem("s_ready"), sem("d_copied"), sem("s_split"), sem("slots_used"))
        d_stored = [sem(f"d_stored{i}") for i in range(2)]
        slots_evac = sem("slots_evac")
        yTp_done, yT_ready, yN_done, yN_evac = sem("yTp_done"), sem("yT_ready"), sem("yN_done"), sem("yN_evac")
        yh_ready, yl_ready = sem("yh_ready"), sem("yl_ready")
        l_done, m1_ready, m0_ready, E1_ready, E0_ready = (
            sem("l_done"), sem("m1_ready"), sem("m0_ready"), sem("E1_ready"), sem("E0_ready"))
        eT_done, eTh_ready, eTl_ready, comb_done = (
            sem("eT_done"), sem("eTh_ready"), sem("eTl_ready"), sem("comb_done"))
        c1_ready, u_ready, fin_ready = sem("c1_ready"), sem("u_ready"), sem("fin_ready")
        dB_loaded = sem("dB_loaded")
        out_stored = [sem(f"out_stored{i}") for i in range(2)]

        N_PAR = 8

        block = ctx.enter_context(nc.Block())

        @block.sync
        def _(sp):
            qw = qkv_w.rearrange("(s p) c -> p s c", p=P)
            sp.dma_start(w_raw, qw).then_inc(par_loaded, 16)
            sp.dma_start(wbc, norm_w.rearrange("(o c) -> o c", o=1).broadcast_to([P, C])).then_inc(par_loaded, 16)
            sp.dma_start(bbc, norm_b.rearrange("(o c) -> o c", o=1).broadcast_to([P, C])).then_inc(par_loaded, 16)
            for g in range(4):
                b, h = g // 2, g % 2
                sp.dma_start(xres[:, b, 8 * h:8 * h + 8, :], x_v[:, b, 8 * h:8 * h + 8, :]).then_inc(x_loaded[g], 16)
            sp.dma_start(phf, phi_v).then_inc(phi_loaded, 16)
            for w in range(2):
                sp.dma_start(Wt[:, w], w_v[w]).then_inc(W_loaded[w], 16)

            def block_io(nb, with_y):
                for j in range(NJ):
                    sp.wait_ge(d_copied, nb * NJ + (j + 3))
                    sp.dma_start(d_dram[j, :, bass.ds(nb * 512, 512)], dS[:, j % 2, :]).then_inc(d_stored[j % 2], 16)
                    if with_y and j % 4 == 3:
                        q = j // 4
                        sp.wait_ge(yTp_done, (nb - 1) * TB + (q + 1))
                        sp.dma_start(Wt[:, q % 2], w_v[bass.ds((nb - 1) * TB + (q + 2), 1)].rearrange(
                            "t p n k e -> p (t n) k e")).then_inc(W_loaded[q % 2], 16)

            block_io(0, False)
            with sp.Fori(1, NB) as nb:
                block_io(nb, True)
            for q in range(2):
                sp.wait_ge(yTp_done, (NB - 1) * TB + q + 1)
                sp.dma_start(Wt[:, q % 2], w_v[(NB - 1) * TB + q + 2]).then_inc(W_loaded[q % 2], 16)

            for i in range(2):
                sp.wait_ge(d_stored[i], 16 * (NB * NJ // 2 + 1))
            sp.wait_ge(slots_used, NB * NJ + 2)
            sp.dma_start(dB, d_dram[0]).then_inc(dB_loaded, 16)

            def store(b, j, fin):
                wait_apart(sp, fin_ready, fin + 2)
                w = 1 - b
                sp.dma_start(out_v[:, b, bass.ds(j, 1), :].rearrange("p j c -> p (j c)"),
                             fo[:, w, :]).then_inc(out_stored[w], 16)

            with sp.Fori(0, NJ - 1) as j:
                sp.wait_ge(m0_ready, j + 1)
                sp.dma_start(dB, d_dram[bass.ds(j + 1, 1)].rearrange("j p n -> p (j n)")).then_inc(dB_loaded, 16)
                store(1, j, 2 * j + 1)
                store(0, j, 2 * j + 2)
            store(1, NJ - 1, 2 * NJ - 1)
            store(0, NJ - 1, 2 * NJ)
            for i in range(2):
                sp.wait_ge(out_stored[i], 16 * (NJ + 1))

        @block.gpsimd
        def _(pool):
            own = Count(pool, pool_own)
            pool.sem_inc(fin_ready, 2)
            own.add(nc.gpsimd.memset(ident[:, :], 0.0))
            own.add(nc.gpsimd.memset(epst[:, 0:2], -0.5))
            own.add(nc.gpsimd.memset(epst[:, 2:3], -1.0))
            own.add(nc.gpsimd.memset(ones[:, :], 1.0))
            own.add(nc.gpsimd.memset(tcount[:, :], float(T)))
            own.wait()
            nc.gpsimd.affine_select(out=ident[:, :], in_=ident[:, :], compare_op=ALU.not_equal, fill=1.0,
                                    base=0, pattern=[[-1, P]], channel_multiplier=1).then_inc(pool_const, 1)

            def rsqrt(o, v):
                n = v.shape[1]
                return nc.gpsimd.tensor_tensor(o, v, epst[:, 0:1].broadcast_to([P, n]), ALU.pow)

            for g in range(4):
                b, h = g // 2, g % 2
                pool.wait_ge(stats_x, g + 1)
                va = ve.rearrange("p (s i) -> p s i", s=2)
                t8 = slice(8 * h, 8 * h + 8)
                v = mvx[:, b, t8, 1]
                own.add(nc.gpsimd.tensor_scalar(va[:, 0], v, EPS, 1.0, ALU.add, ALU.mult))
                own.wait()
                own.add(nc.gpsimd.tensor_scalar(va[:, 1], va[:, 0], EPS, 0.0, ALU.mult, ALU.add))
                own.wait()
                own.add(nc.gpsimd.tensor_tensor(va[:, 1], va[:, 1], v, ALU.add))
                own.wait()
                rsqrt(rx[:, 1, b, t8], va[:, 1]).then_inc(rstd_x, 1)
                own.add(rsqrt(rx[:, 0, b, t8], va[:, 0]))
                own.wait()
                own.add(nc.gpsimd.tensor_tensor(rx[:, 2, b, t8], mvx[:, b, t8, 0], rx[:, 0, b, t8], ALU.mult))
                own.wait()
                nc.gpsimd.tensor_scalar(rx[:, 2, b, t8], rx[:, 2, b, t8], -1.0, 0.0, ALU.mult, ALU.add).then_inc(nx_ready, 1)
                pool.wait_ge(nx_ready, g + 1)
            pool.wait_ge(gmax_in, 1)
            nc.gpsimd.partition_all_reduce(gm[:, 0:1], pm[:, 0:1], P, bass.bass_isa.ReduceOp.max).then_inc(gmax_out, 1)

            pool.wait_ge(abc_ready, 1)

            def bias_row(g):
                pool.wait_ge(x1_ready, g + 1)
                for b in range(B):
                    ins = nc.gpsimd.tensor_tensor(x1a[:, g % 2, :, b, :], x1a[:, g % 2, :, b, :],
                                                  abc[:, b:b + 1, :].broadcast_to([P, GJ, C]), ALU.add)
                ins.then_inc(x1a_ready, 1)

            def norm_terms(mv, r, n, scale):
                own.wait()
                own.add(nc.gpsimd.tensor_scalar(ve[:, 0:8], mv[:, :, 1], EPS, scale ** -2, ALU.add, ALU.mult))
                own.wait()
                own.add(rsqrt(r, ve[:, 0:8]))
                own.wait()
                own.add(nc.gpsimd.tensor_tensor(n, mv[:, :, 0], r, ALU.mult))
                own.wait()
                return nc.gpsimd.tensor_scalar(n, n, -1.0, 0.0, ALU.mult, ALU.add)

            bias_row(0)
            for p in range(NG + 1):
                gx, gy = p, p - 1
                if gy >= 0:
                    pool.wait_ge(mv2_ready, gy + 1)
                    norm_terms(mv2, r3, n3, X_SCALE).then_inc(r3_ready, 1)
                if gx + 1 < NG:
                    bias_row(gx + 1)
                if gy >= 0:
                    pool.wait_ge(x3_ready, gy + 1)
                    nc.gpsimd.tensor_tensor(xd, x3f[:, :, 0, :], x3f[:, :, 1, :], ALU.subtract).then_inc(xd_ready, 1)
                if gx < NG:
                    pool.wait_ge(mvy_ready, gx + 1)
                    norm_terms(mvy, ry, ny[:, 8 * gx:8 * gx + 8], 1.0).then_inc(ry_ready, 1)
                if gy >= 0:
                    pool.wait_ge(x3h_ready, gy + 1)
                    t4 = slice(gy * GJ, gy * GJ + GJ)
                    for b in range(B):
                        ins = nc.gpsimd.tensor_tensor(x3n[:, b, t4, 1, :], x3f[:, :, b, :], x3n[:, b, t4, 0, :],
                                                      ALU.subtract)
                    ins.then_inc(x3l_ready, 1)

            pool.wait_ge(gmax_in, 2)
            nc.gpsimd.partition_all_reduce(gm[:, 1:2], pm[:, 1:2], P, bass.bass_isa.ReduceOp.max).then_inc(gmax_out, 1)
            pool.wait_ge(gmax_in, 3)

            def finish(b, j, seq, n):
                w = 1 - b
                t = tl[:, w, :]
                pool.wait_ge(u_ready, seq + 3)
                own.add(nc.gpsimd.tensor_tensor(t[:, 0:1], zz[:, w, bass.ds(j, 1), 0], zz[:, w, bass.ds(j, 1), 1], ALU.add))
                own.wait()
                own.add(nc.gpsimd.tensor_tensor(t[:, 1:2], t[:, 0:1], epst[:, 2:3], ALU.pow))
                own.wait()
                own.add(nc.gpsimd.tensor_tensor(t[:, 2:3], t[:, 1:2], isg[:, 1:2], ALU.mult))
                own.wait()
                own.add(nc.gpsimd.tensor_tensor(t[:, 3:4], t[:, 2:3], mvC[:, w, 1:2], ALU.mult))
                own.wait()
                own.add(nc.gpsimd.tensor_tensor(t[:, 3:4], t[:, 3:4], t[:, 2:3], ALU.mult))
                own.wait_apart()
                own.add(nc.gpsimd.tensor_scalar(t[:, 3:4], t[:, 3:4], EPS, 1.0, ALU.add, ALU.mult))
                own.wait()
                own.add(rsqrt(t[:, 4:5], t[:, 3:4]))
                own.wait()
                own.add(nc.gpsimd.tensor_tensor(t[:, 5:6], t[:, 4:5], t[:, 2:3], ALU.mult))
                own.wait()
                own.add(nc.gpsimd.tensor_tensor(t[:, 6:7], t[:, 5:6], mvC[:, w, 0:1], ALU.mult))
                own.wait()
                own.add(nc.gpsimd.tensor_tensor(t[:, 7:8], ny[:, bass.ds(2 * j + b, 1)], t[:, 6:7], ALU.subtract))
                own.wait_apart()
                own.add(nc.gpsimd.tensor_scalar(fz[:, w, :], u[:, w, :], t[:, 5:6], t[:, 7:8], ALU.mult, ALU.add))
                own.wait()
                wait_apart(pool, out_stored[w], 16 * n + 16)
                nc.gpsimd.tensor_tensor(fo[:, w, :], fz[:, w, :],
                                        xres[:, b, bass.ds(j, 1), :].rearrange("p j c -> p (j c)"),
                                        ALU.add).then_inc(fin_ready, 1)

            finish(1, 0, 0, 0)
            with pool.Fori(1, NJ) as j:
                own.enter(j - 1, 22)
                finish(0, j - 1, 2 * j - 1, j - 1)
                finish(1, j, 2 * j, j)
                own.leave(NJ - 1)
            finish(0, NJ - 1, 2 * NJ - 1, NJ - 1)

        @block.scalar
        def _(act):
            act.dma_start(wpT, proj_wT.rearrange("(k p) e -> p k e", p=P)).then_inc(par_loaded, 16)
            act.dma_start(qbc, qkv_b).then_inc(par_loaded, 16)
            for b in range(B):
                act.dma_start(pb2[:, b * C:(b + 1) * C], proj_b.rearrange("(o c) -> o c", o=1)).then_inc(par_loaded, 16)
            act.dma_start(bT[:, :, :], ffn_bT.rearrange("(k p) n -> p k n", p=P)).then_inc(par_loaded, 16)
            act.sem_inc(d_copied, 2)

            def copy(o, i, scale=1.0):
                return nc.scalar.activation(o, i, ACT.Copy, scale=scale)

            act.wait_ge(wprod_done, 1)
            copy(G[:, 0, :], bk[0][:, 0:C + 1]).then_inc(wprod_evac, 1)
            copy(G[:, 1, :], bk[1][:, 0:C + 1]).then_inc(wprod_evac, 1)
            copy(U, bk[2][:, :].rearrange("p (k c) -> p k c", k=K)).then_inc(wprod_evac, 1)
            copy(g_row, bk[3][0:1, 0:C + 1]).then_inc(wprod_evac, 1)
            copy(u_row, psL[0:1, 1536:1536 + C]).then_inc(wprod_evac, 1)
            def x1(g, half):
                if half == 0:
                    act.wait_ge(nx_ready, 3 + g // 2)
                    if g >= 2:
                        act.wait_ge(y_read, GJ * (g - 1))
                for jj in (2 * half, 2 * half + 1):
                    for b in range(B):
                        t = g * GJ + jj
                        ins = nc.scalar.activation(x1a[:, g % 2, jj, b, :], xres[:, b, t, :], ACT.Identity,
                                                   bias=rx[:, 2, b, t:t + 1], scale=rx[:, 0, b, t:t + 1])
                if half == 1:
                    ins.then_inc(x1_ready, 1)

            for b in range(B):
                if b == 1:
                    x1(0, 0)
                    x1(0, 1)
                act.wait_ge(xh_used, NJ * (b + 1))
                for k in range(K):
                    copy(S_sb[:, b, k, :], psL[:, (b * K + k) * 512:(b * K + k) * 512 + C + 1]).then_inc(S_evac, 1)
            act.wait_ge(crow_done, 1)
            copy(c_row, bk[3][0:1, :]).then_inc(crow_evac, 1)
            act.wait_ge(R_done, 1)
            for b in range(B):
                copy(R[:, b], bk[b][:, :].rearrange("p (k c) -> p k c", k=K)).then_inc(R_evac, 1)
            copy(r_row, bk[2][0:1, :]).then_inc(R_evac, 1)
            act.wait_ge(A_done, 1)
            for b in range(B):
                copy(A_sb[:, b], psL[:, b * 512:(b + 1) * 512].rearrange("p (k c) -> p k c", k=K),
                     scale=1.0 / math.sqrt(C)).then_inc(A_evac, 1)
            act.wait_ge(abc_done, 1)
            copy(abc[:, :, :], psL[:, 1024:1536].rearrange("p (b c) -> p b c", b=B)).then_inc(abc_ready, 1)

            def dispatch(nb, j):
                act.wait_ge(d_done, nb * NJ + (j + 1))
                act.wait_ge(s_split, nb * NJ + (j + 1))
                for s in range(B):
                    ins = nc.scalar.activation(sF[:, j % 2, s, :], bk[j % 2][:, :], ACT.Sigmoid, scale=kap[:, s:s + 1])
                ins.then_inc(s_ready, 1)
                act.wait_ge(d_stored[j % 2], nb * (8 * NJ) + (16 * (j // 2) + 16))
                copy(dS[:, j % 2, :], bk[j % 2][:, :]).then_inc(d_copied, 1)

            def block_act(nb):
                for j in range(NJ):
                    dispatch(nb, j)
                    if j % 4 == 1 and j > 1:
                        y_evac(nb - 1, (j - 5) // 4)
                y_evac(nb - 1, 3)

            def y_evac(yb_, q):
                act.wait_ge(yN_done, yb_ * TB + (q + 2))
                copy(yf[:, :, bass.ds(yb_ * TB + q, 1), :].rearrange("p b t c -> p b (t c)"),
                     bk[3][:, :].rearrange("p (b c) -> p b c", b=B)).then_inc(yN_evac, 1)

            def xT_evac(t):
                act.wait_ge(hT_done, t + 1)
                if t >= 2:
                    act.wait_ge(y_done, t - 1)
                copy(xT[:, t % 2, :], bk[2][:, :]).then_inc(hT_evac, 1)

            def x3_hiT(t):
                act.wait_ge(x3T_done, t + 1)
                pv = bk[2 + t % 2][:, :].rearrange("p (w k t) -> p w k t", w=2, k=K)
                copy(xT1[:, 0, :, t * P:(t + 1) * P], pv[:, 0])
                copy(xdT[:, 0, :, t * P:(t + 1) * P], pv[:, 1]).then_inc(x3Th_ready, 1)

            for p in range(NG + 2):
                gx, gy, gz = p, p - 1, p - 2
                X, Y, Z = gx < NG, 0 <= gy < NG, gz >= 0
                tx, ty, tz = gx * GJ, gy * GJ, gz * GJ
                if gz == 0:
                    act.wait_ge(phi_split, 1)
                if Z:
                    dispatch(0, tz)
                if X:
                    xT_evac(tx)
                if Z:
                    dispatch(0, tz + 1)
                if X:
                    xT_evac(tx + 1)
                    if gx + 1 < NG:
                        x1(gx + 1, 0)
                    xT_evac(tx + 2)
                if Z:
                    dispatch(0, tz + 2)
                if X:
                    if gx + 1 < NG:
                        x1(gx + 1, 1)
                    xT_evac(tx + 3)
                if Y:
                    act.wait_ge(r3_ready, gy + 1)
                    if gy:
                        act.wait_ge(x3T_done, ty)
                        act.wait_ge(x3l_ready, gy)
                    for i in range(8):
                        ins = nc.scalar.activation(x3f[:, i // 2, i % 2, :], xres[:, i % 2, ty + i // 2, :], ACT.Identity,
                                                   bias=n3[:, i:i + 1], scale=r3[:, i:i + 1])
                    ins.then_inc(x3_ready, 1)
                if Z:
                    dispatch(0, tz + 3)
                if Y:
                    act.wait_ge(x3_ready, gy + 1)
                    for b in range(B):
                        ins = copy(x3n[:, b, ty:ty + GJ, 0, :], x3f[:, :, b, :])
                    ins.then_inc(x3h_ready, 1)
                    for jj in range(GJ):
                        x3_hiT(ty + jj)

            with act.Fori(1, NB) as nb:
                block_act(nb)
            for q in range(TB):
                y_evac(NB - 1, q)

            act.wait_ge(gmax_in, 3)
            act.wait_ge(slots_used, NB * NJ + 2)
            act.wait_ge(yN_evac, NB * TB + 1)
            for b in (1, 0):
                for h in range(2):
                    t8 = slice(8 * h, 8 * h + 8)
                    nc.scalar.activation(yhl[:, b, t8, 0, :], yf[:, b, t8, :], ACT.Identity,
                                         scale=sg[:, 1:2]).then_inc(yh_ready, 1)

            def hi(m, gq):
                act.wait_ge(eT_done, m + 1)
                act.wait_ge(comb_done, m + 1)
                copy(eT[:, gq, 0, :], bk[gq % 2][:, :]).then_inc(eTh_ready, 1)

            def expo(b, j, half):
                src, dst = (psL, E1) if b else (l0, E0)
                w = 1 - b
                nc.scalar.activation(dst[:, 1024 * half:1024 * half + 1024], src[:, 1024 * half:1024 * half + 1024],
                                     ACT.Exp, bias=ebias[:, w:w + 1], scale=kap[:, 0:1],
                                     accum_out=zz[:, w, bass.ds(j, 1), half]).then_inc(
                                         E1_ready if b else E0_ready, 1)

            def c1_copy(b, seq, m_end):
                act.wait_ge(comb_done, m_end + 4)
                act.wait_ge(u_ready, seq + 1)
                copy(c1[:, 1 - b, :], bk[3 - b][:, 256:512]).then_inc(c1_ready, 1)

            def comb_act(j, first):
                if not first:
                    hi(8 * j - 4, 0)
                    hi(8 * j - 3, 1)
                    c1_copy(1, 2 * j - 2, 8 * j - 4)
                    hi(8 * j - 2, 2)
                act.wait_ge(m1_ready, j + 1)
                expo(1, j, 0)
                if not first:
                    hi(8 * j - 1, 3)
                expo(1, j, 1)
                hi(8 * j, 0)
                hi(8 * j + 1, 1)
                act.wait_ge(m0_ready, j + 1)
                expo(0, j, 0)
                hi(8 * j + 2, 2)
                expo(0, j, 1)
                if not first:
                    c1_copy(0, 2 * j - 1, 8 * j)
                hi(8 * j + 3, 3)

            comb_act(0, True)
            with act.Fori(1, NJ) as j:
                comb_act(j, False)
            hi(8 * NJ - 4, 0)
            hi(8 * NJ - 3, 1)
            c1_copy(1, 2 * NJ - 2, 8 * NJ - 4)
            hi(8 * NJ - 2, 2)
            hi(8 * NJ - 1, 3)
            c1_copy(0, 2 * NJ - 1, 8 * NJ)

        @block.vector
        def _(dve):
            own = Count(dve, dve_own)
            V = nc.vector
            dve.sem_inc(s_split, 2)
            dve.sem_inc(slots_evac, 4)
            dve.sem_inc(eTl_ready, 2)
            dve.sem_inc(u_ready, 2)
            for i in range(2):
                dve.sem_inc(d_stored[i], 16)
                dve.sem_inc(out_stored[i], 16)

            own.add(V.memset(xbuf[:, :, C:C + 1], 1.0))
            dve.wait_ge(par_loaded, 16 * N_PAR)
            for s in range(KS):
                own.add(V.tensor_tensor_reduce(junk, w_raw[:, s, :], bbc, 1.0, 0.0, ALU.mult, ALU.add, bcol[:, s:s + 1]))
                own.wait()
            own.add(V.tensor_tensor(w_aug[:, :, 0:C], w_raw, wbc.unsqueeze(1).broadcast_to([P, KS, C]), ALU.mult))
            V.tensor_tensor(w_aug[:, :, C], bcol, qbc, ALU.add).then_inc(waug_ready, 1)

            for g in range(4):
                b, h = g // 2, g % 2
                dve.wait_ge(x_loaded[g], 16)
                if g:
                    own.wait()
                for i in range(8):
                    own.add(V.bn_stats(stat[:, 0, i, :], xres[:, b, 8 * h + i, :]))
                own.wait()
                for i in range(7):
                    own.add(V.bn_aggr(mvx[:, b, 8 * h + i, :], stat[:, 0, i, :]))
                V.bn_aggr(mvx[:, b, 8 * h + 7, :], stat[:, 0, 7, :]).then_inc(stats_x, 1)
                dve.wait_ge(rstd_x, g + 1)
                own.wait()
                for i in range(8):
                    t = 8 * g + i
                    if t >= 4:
                        dve.wait_ge(xh_used, t - 3)
                    j = 8 * h + i
                    V.tensor_scalar(xbuf[:, t % 4, 0:C], xres[:, b, j, :], mvx[:, b, j, 0:1], rx[:, 1, b, j:j + 1],
                                    ALU.subtract, ALU.mult).then_inc(xh_ready, 1)

            def pow2_scale(i):
                c = slice(i, i + 1)
                own.add(V.tensor_scalar(gm[:, c], gm[:, c], 2.0 ** -100, None, ALU.max))
                own.wait()
                own.add(V.tensor_scalar(gm[:, c].bitcast(I32), gm[:, c].bitcast(I32), 0x7F800000, None, ALU.bitwise_and))
                own.wait()
                own.add(V.tensor_scalar(isg[:, c], gm[:, c], 2.0 ** -TOP_EXP, None, ALU.mult))
                own.wait()
                own.add(V.reciprocal(sg[:, c], isg[:, c]))
                own.wait()

            dve.wait_ge(phi_loaded, 16)
            V.tensor_reduce(pm[:, 0:1], phf.rearrange("p k n -> p (k n)"), AX_X, ALU.max,
                            apply_absolute_value=True).then_inc(gmax_in, 1)
            dve.wait_ge(gmax_out, 1)
            pow2_scale(0)
            own.add(V.tensor_scalar(kap[:, 0:1], isg[:, 0:1], 1.0 / X_SCALE, None, ALU.mult))
            own.add(V.tensor_scalar(kap[:, 1:2], isg[:, 0:1], -1.0 / X_SCALE, None, ALU.mult))
            own.add(V.tensor_scalar(phs[:, 0], phf, sg[:, 0:1], None, ALU.mult))
            own.wait()
            V.scalar_tensor_tensor(phs[:, 1].rearrange("p k n -> p (k n)"), phf.rearrange("p k n -> p (k n)"),
                                   sg[:, 0:1], phs[:, 0].rearrange("p k n -> p (k n)"), ALU.mult,
                                   ALU.subtract).then_inc(phi_split, 1)

            dve.wait_ge(A_done, 1)
            V.scalar_tensor_tensor(a_row, bk[3][0:1, :], 1.0 / math.sqrt(C), pb2, ALU.mult, ALU.add).then_inc(arow_ready, 1)

            dve.wait_ge(xh_used, B * NJ)

            def xhat(t):
                if t >= 2:
                    dve.wait_ge(hT_done, t - 1)
                for b in range(B):
                    ins = V.tensor_scalar(xbuf[:, 2 * (t % 2) + b, 0:C], xres[:, b, t, :],
                                          mvx[:, b, t, 0:1], rx[:, 1, b, t:t + 1], ALU.subtract, ALU.mult)
                ins.then_inc(xh_ready, 1)

            def attn(t):
                dve.wait_ge(y_done, t + 1)
                if t % GJ == 0:
                    dve.wait_ge(x1a_ready, t // GJ + 1)
                V.tensor_tensor(yb[:, t % GJ], bk[3][:, :].rearrange("p (b c) -> p b c", b=B),
                                x1a[:, t // GJ % 2, t % GJ], ALU.add).then_inc(y_read, 1)

            def statistics(w, tile, mv):
                for i in range(8):
                    own.add(V.bn_stats(stat[:, w, i, :], tile(i)))
                own.wait()
                for i in range(8):
                    ins = V.bn_aggr(mv[:, i, :], stat[:, w, i, :])
                return ins

            def x3_loT(t):
                dve.wait_ge(x3Th_ready, t + 1)
                pv = bk[2 + t % 2][:, :].rearrange("p (w k t) -> p w k t", w=2, k=K)
                cols = slice(t * P, (t + 1) * P)
                V.tensor_tensor(xT1[:, 1, :, cols], pv[:, 0], xT1[:, 0, :, cols], ALU.subtract)
                V.tensor_tensor(xdT[:, 1, :, cols], pv[:, 1], xdT[:, 0, :, cols], ALU.subtract).then_inc(x3Tl_ready, 1)

            def split(nb, j):
                dve.wait_ge(s_ready, nb * NJ + (j + 1))
                dve.wait_ge(slots_used, nb * NJ + (j + 1))
                own.add(V.tensor_scalar(shl[:, j % 2, 0], sF[:, j % 2], S_SCALE, None, ALU.mult))
                own.wait()
                V.scalar_tensor_tensor(shl[:, j % 2, 1], sF[:, j % 2], S_SCALE, shl[:, j % 2, 0],
                                       ALU.mult, ALU.subtract).then_inc(s_split, 1)

            for p in range(NG + 2):
                gx, gy, gz = p, p - 1, p - 2
                X, Y, Z = gx < NG, 0 <= gy < NG, gz >= 0
                tx, ty, tz = gx * GJ, gy * GJ, gz * GJ
                if X:
                    xhat(tx)
                    xhat(tx + 1)
                if Z:
                    split(0, tz)
                if Y:
                    dve.wait_ge(ry_ready, gy + 1)
                    for i in range(8):
                        own.add(V.scalar_tensor_tensor(xres[:, i % 2, ty + i // 2, :], yb[:, i // 2, i % 2, :], ry[:, i:i + 1],
                                                       xres[:, i % 2, ty + i // 2, :], ALU.mult, ALU.add))
                    own.wait()
                if X:
                    attn(tx)
                    xhat(tx + 2)
                if Y:
                    if gy:
                        dve.wait_ge(r3_ready, gy)
                    statistics(1, lambda i: xres[:, i % 2, ty + i // 2, :], mv2).then_inc(mv2_ready, 1)
                if X:
                    attn(tx + 1)
                    xhat(tx + 3)
                if Z:
                    split(0, tz + 1)
                if X:
                    attn(tx + 2)
                    attn(tx + 3)
                    dve.wait_ge(y_read, tx + GJ)
                    statistics(0, lambda i: yb[:, i // 2, i % 2, :], mvy).then_inc(mvy_ready, 1)
                if Z:
                    split(0, tz + 2)
                if Y:
                    x3_loT(ty)
                    x3_loT(ty + 1)
                if Z:
                    split(0, tz + 3)
                if Y:
                    x3_loT(ty + 2)
                    x3_loT(ty + 3)
            dve.wait_ge(slots_used, NJ + 2)

            def block_dve(nb):
                for j in range(NJ):
                    split(nb, j)
                    if j % 4 == 2:
                        y_bias(nb - 1, j // 4)
                dve.wait_ge(slots_used, nb * NJ + (NJ + 2))
                slots_out(nb)

            def slots_out(nb):
                for k in range(K):
                    for b in range(B):
                        i = k * B + b
                        V.tensor_scalar(slT[:, k, :, b, :],
                                        psL[:, i * 512:(i + 1) * 512].rearrange("p (n q) -> p n q", q=Q),
                                        1.0 / (X_SCALE * S_SCALE), None, ALU.mult).then_inc(slots_evac, 1)

            def y_bias(yb_, q):
                dve.wait_ge(yTp_done, yb_ * TB + (q + 1))
                dve.wait_ge(yN_done, yb_ * TB + (q + 1))
                own.wait()
                for e in range(K):
                    V.tensor_tensor(
                        yT[:, e].rearrange("p b (n q) -> p b n q", q=Q),
                        bk[2][:, e * 256:(e + 1) * 256].rearrange("p (n b q) -> p b n q", n=EP, b=B),
                        bT[:, e, bass.ds((yb_ * TB + q) * EP, EP)].unsqueeze(1).unsqueeze(3).broadcast_to([P, B, EP, Q]),
                        ALU.add).then_inc(yT_ready, 1)
                dve.wait_ge(yT_ready, (yb_ * TB + q) * 2 + 4)
                own.add(V.tensor_reduce(ymx[:, bass.ds(yb_ * TB + q, 1)], yT.rearrange("p e b n -> p (e b n)"),
                                        AX_X, ALU.max, apply_absolute_value=True))

            slots_out(0)
            with dve.Fori(1, NB) as nb:
                own.enter(nb - 1, NJ + TB)
                block_dve(nb)
                own.leave(NB - 1)
            for q in range(TB):
                y_bias(NB - 1, q)
            own.wait()
            V.tensor_reduce(pm[:, 1:2], ymx, AX_X, ALU.max).then_inc(gmax_in, 1)
            dve.wait_ge(gmax_out, 2)
            pow2_scale(1)
            dve.sem_inc(gmax_in, 1)

            def lo(m, gq):
                dve.wait_ge(eTh_ready, m + 1)
                V.tensor_tensor(eT[:, gq, 1, :], bk[gq % 2][:, :], eT[:, gq, 0, :], ALU.subtract).then_inc(eTl_ready, 1)

            def maxima(j, w, last):
                own.wait()
                own.add(V.tensor_reduce(m1[:, w:w + 1], m4[:, 4 * w:4 * w + 4], AX_X, ALU.max))
                own.wait()
                V.tensor_scalar(ebias[:, w:w + 1], m1[:, w:w + 1], kap[:, 1:2], E_LOG, ALU.mult, ALU.add).then_inc(last, 1)

            def add_max(j, kb):
                c = slice(512 * kb, 512 * kb + 512)
                own.add(V.tensor_tensor_reduce(l0[:, c], psL[:, c], dB[:, c], 1.0, -3.0e38, ALU.add, ALU.max,
                                               m4[:, 4 + kb:5 + kb]))

            def tail(b, seq):
                w = 1 - b
                dve.wait_ge(c1_ready, seq + 1)
                own.add(V.tensor_tensor(u[:, w, :], bk[3 - b][:, 0:256], c1[:, w, :], ALU.add))
                own.wait()
                own.add(V.bn_stats(stat[:, 0, w, :], u[:, w, :]))
                own.wait_apart()
                V.bn_aggr(mvC[:, w, :], stat[:, 0, w, :]).then_inc(u_ready, 1)

            def comb_dve(j, first):
                if not first:
                    lo(8 * j - 4, 0)
                    lo(8 * j - 3, 1)
                    dve.wait_ge(fin_ready, 2 * j - 1)
                    tail(1, 2 * j - 2)
                for kb in range(4):
                    dve.wait_ge(l_done, 4 * j + kb + 1)
                    own.add(V.tensor_reduce(m4[:, kb:kb + 1], psL[:, 512 * kb:512 * kb + 512], AX_X, ALU.max))
                maxima(j, 0, m1_ready)
                if not first:
                    lo(8 * j - 2, 2)
                    dve.wait_ge(E0_ready, 2 * j)
                dve.wait_ge(dB_loaded, 16 * j + 16)
                wait_apart(dve, E1_ready, 2 * j + 1)
                add_max(j, 0)
                add_max(j, 1)
                if not first:
                    lo(8 * j - 1, 3)
                wait_apart(dve, E1_ready, 2 * j + 2)
                add_max(j, 2)
                add_max(j, 3)
                maxima(j, 1, m0_ready)
                for gq in range(3):
                    lo(8 * j + gq, gq)
                if not first:
                    dve.wait_ge(fin_ready, 2 * j)
                    tail(0, 2 * j - 1)
                lo(8 * j + 3, 3)

            def y_lo():
                for i, (b, h) in enumerate(((1, 0), (1, 1), (0, 0), (0, 1))):
                    t8 = slice(8 * h, 8 * h + 8)
                    dve.wait_ge(yh_ready, i + 1)
                    V.scalar_tensor_tensor(yhl[:, b, t8, 1, :], yf[:, b, t8, :], sg[:, 1:2], yhl[:, b, t8, 0, :],
                                           ALU.mult, ALU.subtract).then_inc(yl_ready, 1)

            y_lo()
            own.enter(0, 10)
            comb_dve(0, True)
            own.leave(1)
            with dve.Fori(1, NJ) as j:
                own.enter(j - 1, 10 + 4)
                comb_dve(j, False)
                own.leave(NJ - 1)
            lo(8 * NJ - 4, 0)
            lo(8 * NJ - 3, 1)
            dve.wait_ge(fin_ready, 2 * NJ - 1)
            tail(1, 2 * NJ - 2)
            lo(8 * NJ - 2, 2)
            lo(8 * NJ - 1, 3)
            dve.wait_ge(fin_ready, 2 * NJ)
            tail(0, 2 * NJ - 1)

        @block.tensor
        def _(pe):
            mm = nc.tensor.matmul
            pe.sem_inc(slots_used, 2)
            pe.sem_inc(comb_done, 4)

            pe.wait_ge(waug_ready, 1)
            wq, wk, wv = w_aug[:, 0:K], w_aug[:, K:2 * K], w_aug[:, 2 * K:3 * K]
            for i in range(K):
                for k in range(K):
                    mm(bk[i][:, 0:C + 1], wk[:, k, i * P:(i + 1) * P], wq[:, k, :], start=(k == 0), stop=(k == K - 1))
            for i in range(K):
                for k in range(K):
                    mm(bk[2][:, i * C:(i + 1) * C], wv[:, k, i * P:(i + 1) * P], wpT[:, k, :], start=(k == 0), stop=(k == K - 1))
            for k in range(K):
                mm(bk[3][0:1, 0:C + 1], wk[:, k, C:C + 1], wq[:, k, :], start=(k == 0), stop=(k == K - 1))
            for k in range(K):
                ins = mm(psL[0:1, 1536:1536 + C], wv[:, k, C:C + 1], wpT[:, k, :], start=(k == 0), stop=(k == K - 1))
            ins.then_inc(wprod_done, 1)

            for b in range(B):
                if b == 1:
                    pe.wait_ge(wprod_evac, 5)
                for j in range(NJ):
                    t = b * NJ + j
                    pe.wait_ge(xh_ready, t + 1)
                    for k in range(K):
                        o = (b * K + k) * 512
                        ins = mm(psL[:, o:o + C + 1], xbuf[:, t % 4, k * P:(k + 1) * P], xbuf[:, t % 4, :],
                                 start=(j == 0), stop=(j == NJ - 1))
                    ins.then_inc(xh_used, 1)

            pe.wait_ge(pool_const, 1)
            pe.wait_ge(S_evac, 4)
            for b in range(B):
                for k in range(K):
                    ins = mm(bk[3][0:1, b * C + k * P:b * C + (k + 1) * P], S_sb[:, b, k, C:C + 1], ident[:, :],
                             start=True, stop=True)
            ins.then_inc(crow_done, 1)
            for b in range(B):
                for i in range(K):
                    for k in range(K):
                        mm(bk[b][:, i * C:(i + 1) * C], S_sb[:, b, k, i * P:(i + 1) * P], U[:, k, :], start=(k == 0), stop=False)
                    if b == 0 and i == 0:
                        pe.wait_ge(crow_evac, 1)
                    mm(bk[b][:, i * C:(i + 1) * C], c_row[:, b * C + i * P:b * C + (i + 1) * P], u_row, start=False, stop=True)
            for b in range(B):
                for k in range(K):
                    mm(bk[2][0:1, b * C:(b + 1) * C], S_sb[:, b, k, C:C + 1], U[:, k, :], start=(k == 0), stop=False)
                ins = mm(bk[2][0:1, b * C:(b + 1) * C], tcount[:, :], u_row, start=False, stop=True)
            ins.then_inc(R_done, 1)
            pe.wait_ge(R_evac, 3)
            for b in range(B):
                for i in range(K):
                    for k in range(K):
                        mm(psL[:, b * 512 + i * C:b * 512 + (i + 1) * C], G[:, k, i * P:(i + 1) * P], R[:, b, k, :], start=(k == 0), stop=False)
                    mm(psL[:, b * 512 + i * C:b * 512 + (i + 1) * C], g_row[:, i * P:(i + 1) * P], r_row[:, b * C:(b + 1) * C], start=False, stop=True)
            for b in range(B):
                for k in range(K):
                    mm(bk[3][0:1, b * C:(b + 1) * C], G[:, k, C:C + 1], R[:, b, k, :], start=(k == 0), stop=False)
                ins = mm(bk[3][0:1, b * C:(b + 1) * C], g_row[:, C:C + 1], r_row[:, b * C:(b + 1) * C], start=False, stop=True)
            ins.then_inc(A_done, 1)
            pe.wait_ge(arow_ready, 1)
            mm(psL[:, 1024:1536], ones[:, :], a_row, start=True, stop=True).then_inc(abc_done, 1)
            pe.wait_ge(A_evac, 2)
            pe.wait_ge(abc_ready, 1)

            def h_transpose(t):
                pe.wait_ge(xh_ready, B * NJ + t + 1)
                if t:
                    pe.wait_ge(hT_evac, t)
                if t % GJ == 0 and t >= 2 * GJ:
                    pe.wait_ge(x3Tl_ready, t - 2 * GJ + 3)
                for b in range(B):
                    for k in range(K):
                        i = b * K + k
                        ins = nc.tensor.transpose(bk[2][:, i * P:(i + 1) * P],
                                                  xbuf[:, 2 * (t % 2) + b, k * P:(k + 1) * P], ident[:, :])
                ins.then_inc(hT_done, 1)

            def h_product(t):
                pe.wait_ge(hT_evac, t + 1)
                if t:
                    pe.wait_ge(y_read, t)
                if t % GJ == 0 and t >= 2 * GJ:
                    pe.wait_ge(x3Tl_ready, t - 2 * GJ + 4)
                for b in range(B):
                    for k in range(K):
                        i = b * K + k
                        ins = mm(bk[3][:, b * C:(b + 1) * C], xT[:, t % 2, i * P:(i + 1) * P],
                                 A_sb[:, b, k, :], start=(k == 0), stop=(k == K - 1))
                ins.then_inc(y_done, 1)

            def x3_transpose(t):
                jj = t % GJ
                if jj == 0:
                    pe.wait_ge(xd_ready, t // GJ + 1)
                    pe.wait_ge(hT_evac, min(NJ, t + 2 * GJ))
                if jj == 1:
                    pe.wait_ge(y_read, min(NJ, t - 1 + 2 * GJ))
                if t >= 2:
                    pe.wait_ge(x3Tl_ready, t - 1)
                for w in range(2):
                    for k in range(K):
                        src = xd[:, jj, k * P:(k + 1) * P] if w else x3f[:, jj, 1, k * P:(k + 1) * P]
                        o = (w * K + k) * P
                        ins = nc.tensor.transpose(bk[2 + t % 2][:, o:o + P], src, ident[:, :])
                ins.then_inc(x3T_done, 1)

            def d_tile(nb, j):
                pe.wait_ge(d_copied, nb * NJ + (j + 1))
                for k in range(K):
                    for hx, hp in ((0, 0), (0, 1), (1, 0)):
                        ins = mm(bk[j % 2][:, :], xdT[:, hx, k, j * P:(j + 1) * P], phs[:, hp, k, bass.ds(nb * 512, 512)],
                                 start=(k == 0 and hx + hp == 0), stop=(k == K - 1 and hx == 1))
                ins.then_inc(d_done, 1)

            def slots(nb, j):
                pe.wait_ge(s_split, nb * NJ + (j + 3))
                if j == 0:
                    pe.wait_ge(slots_evac, nb * 4 + 4)
                for k in range(K):
                    for b in range(B):
                        i = k * B + b
                        for hx, hs in ((0, 0), (0, 1), (1, 0)):
                            ins = mm(psL[:, i * 512:(i + 1) * 512], x3n[:, b, j, hx, k * P:(k + 1) * P],
                                     shl[:, j % 2, hs, b, :], start=(j == 0 and hx + hs == 0), stop=(j == NJ - 1 and hx == 1))
                ins.then_inc(slots_used, 1)

            def y_product(yb_, q):
                pe.wait_ge(W_loaded[q % 2], yb_ * (8 * TB) + (16 * (q // 2) + 16))
                if q == 0:
                    pe.wait_ge(slots_evac, yb_ * 4 + 8)
                pe.wait_ge(yT_ready, (yb_ * TB + q) * 2 + YT0)
                for n in range(EP):
                    for e in range(K):
                        for k in range(K):
                            o = e * 256 + n * 64
                            ins = mm(bk[2][:, o:o + 64], Wt[:, q % 2, n, k, e * P:(e + 1) * P],
                                     slT[:, k, q * EP + n].rearrange("p b q -> p (b q)"), start=(k == 0), stop=(k == K - 1))
                ins.then_inc(yTp_done, 1)

            def y_turn(yb_, q):
                pe.wait_ge(yT_ready, (yb_ * TB + q) * 2 + YT0 + 2)
                pe.wait_ge(yN_evac, yb_ * TB + q + 1)
                for b in range(B):
                    for e in range(K):
                        o = b * 256 + e * P
                        ins = nc.tensor.transpose(bk[3][:, o:o + P], yT[:, e, b, :], ident[:, :])
                ins.then_inc(yN_done, 1)

            YT0 = 2
            pe.sem_inc(yT_ready, 2)
            pe.sem_inc(yN_evac, 1)
            pe.sem_inc(yN_done, 1)

            for p in range(NG + 2):
                gx, gy, gz = p, p - 1, p - 2
                X, Y, Z = gx < NG, 0 <= gy < NG, gz >= 0
                tx, ty, tz = gx * GJ, gy * GJ, gz * GJ
                if Z:
                    pe.wait_ge(x3Tl_ready, tz + 1)
                    d_tile(0, tz)
                if X:
                    h_transpose(tx)
                if Z:
                    pe.wait_ge(x3Tl_ready, tz + 4)
                    d_tile(0, tz + 1)
                if X:
                    h_product(tx)
                    h_transpose(tx + 1)
                if Z:
                    pe.wait_ge(x3l_ready, gz + 1)
                    slots(0, tz)
                if X:
                    h_product(tx + 1)
                    h_transpose(tx + 2)
                if Z:
                    d_tile(0, tz + 2)
                if X:
                    h_product(tx + 2)
                    h_transpose(tx + 3)
                if Z:
                    slots(0, tz + 1)
                if X:
                    h_product(tx + 3)
                if Z:
                    d_tile(0, tz + 3)
                    slots(0, tz + 2)
                if Y:
                    x3_transpose(ty)
                    x3_transpose(ty + 1)
                if Z:
                    slots(0, tz + 3)
                if Y:
                    x3_transpose(ty + 2)
                    x3_transpose(ty + 3)

            def block_pe(nb):
                d_tile(nb, 0)
                d_tile(nb, 1)
                for j in range(NJ):
                    slots(nb, j)
                    if j % 4 == 1:
                        y_product(nb - 1, j // 4)
                    if j + 2 < NJ:
                        d_tile(nb, j + 2)
                    if j % 4 == 3:
                        y_turn(nb - 1, j // 4)

            with pe.Fori(1, NB) as nb:
                block_pe(nb)

            def logits(j, kbs):
                for kb in kbs:
                    for k in range(K):
                        for hx, hp in ((0, 0), (0, 1), (1, 0)):
                            ins = mm(psL[:, kb * 512:(kb + 1) * 512], xT1[:, hx, k, bass.ds(j * P, P)],
                                     phs[:, hp, k, kb * 512:(kb + 1) * 512],
                                     start=(k == 0 and hx + hp == 0), stop=(k == K - 1 and hx == 1))
                    ins.then_inc(l_done, 1)

            def turn(b, j, m, gq):
                pe.wait_ge(E1_ready if b else E0_ready, 2 * j + 1 + gq // 2)
                pe.wait_ge(eTl_ready, m + 1)
                E = E1 if b else E0
                for i in range(4):
                    o = gq * 512 + i * P
                    ins = nc.tensor.transpose(bk[gq % 2][:, i * P:(i + 1) * P], E[:, o:o + P], ident[:, :])
                ins.then_inc(eT_done, 1)

            def high(b, seq, m, gq):
                pe.wait_ge(eTh_ready, m + 1)
                if gq == 0:
                    pe.wait_ge(u_ready, seq + 1)
                for i in range(4):
                    t = gq * 4 + i
                    mm(bk[3 - b][:, :], eT[:, gq, 0, i * P:(i + 1) * P], yhl[:, b, t].rearrange("p h c -> p (h c)"),
                       start=(t == 0), stop=False)

            def low(b, m, gq):
                pe.wait_ge(eTl_ready, m + 3)
                for i in range(4):
                    t = gq * 4 + i
                    ins = mm(bk[3 - b][:, 256:512], eT[:, gq, 1, i * P:(i + 1) * P], yhl[:, b, t, 0, :],
                             start=False, stop=(t == NT - 1))
                ins.then_inc(comb_done, 1)

            def comb_pe(j, first):
                m = 8 * j
                if first:
                    turn(1, j, m, 0)
                    turn(1, j, m + 1, 1)
                else:
                    turn(0, j - 1, m - 3, 1)
                    low(1, m - 5, 3)
                    logits(j, range(4))
                    pe.wait_ge(yl_ready, 4)
                    high(0, 2 * j - 1, m - 4, 0)
                    turn(0, j - 1, m - 2, 2)
                    high(0, 2 * j - 1, m - 3, 1)
                    turn(0, j - 1, m - 1, 3)
                    low(0, m - 4, 0)
                    high(0, 2 * j - 1, m - 2, 2)
                    turn(1, j, m, 0)
                    low(0, m - 3, 1)
                    high(0, 2 * j - 1, m - 1, 3)
                    turn(1, j, m + 1, 1)
                    low(0, m - 2, 2)
                if first:
                    pe.wait_ge(yl_ready, 1)
                high(1, 2 * j, m, 0)
                turn(1, j, m + 2, 2)
                if not first:
                    low(0, m - 1, 3)
                high(1, 2 * j, m + 1, 1)
                turn(1, j, m + 3, 3)
                low(1, m, 0)
                if first:
                    pe.wait_ge(yl_ready, 2)
                high(1, 2 * j, m + 2, 2)
                turn(0, j, m + 4, 0)
                low(1, m + 1, 1)
                high(1, 2 * j, m + 3, 3)
                low(1, m + 2, 2)

            for q in range(TB):
                y_product(NB - 1, q)
                logits(0, (q,))
                y_turn(NB - 1, q)
            comb_pe(0, True)
            with pe.Fori(1, NJ) as j:
                comb_pe(j, False)
            m = 8 * NJ
            turn(0, NJ - 1, m - 3, 1)
            low(1, m - 5, 3)
            high(0, 2 * NJ - 1, m - 4, 0)
            turn(0, NJ - 1, m - 2, 2)
            high(0, 2 * NJ - 1, m - 3, 1)
            turn(0, NJ - 1, m - 1, 3)
            low(0, m - 4, 0)
            high(0, 2 * NJ - 1, m - 2, 2)
            low(0, m - 3, 1)
            high(0, 2 * NJ - 1, m - 1, 3)
            low(0, m - 2, 2)
            low(0, m - 1, 3)


def kernel(**inputs):
    import numpy as np
    import concourse.bacc as bacc
    from concourse.bass_utils import run_bass_kernel_spmd

    nc = bacc.Bacc("TRN2", target_bir_lowering=False, num_devices=1)
    laid = {
        "x": inputs["L0_attn_x"],
        "norm_w": inputs["L0_attn_norm_w"],
        "norm_b": inputs["L0_attn_norm_b"],
        "qkv_w": inputs["L0_attn_qkv_w"],
        "qkv_b": np.reshape(inputs["L0_attn_qkv_b"], (-1, 128)).T,
        "proj_wT": np.transpose(inputs["L0_attn_proj_w"]),
        "proj_b": inputs["L0_attn_proj_b"],
        "phi": inputs["L0_ffn_phi"],
        "ffn_w": inputs["L0_ffn_W"],
        "ffn_bT": np.transpose(inputs["L0_ffn_b"]),
    }
    arrays, args = {}, []
    for name, a in laid.items():
        a = np.ascontiguousarray(a)
        arrays[f"in_{name}"] = a
        args.append(nc.dram_tensor(f"in_{name}", a.shape, mybir.dt.from_np(a.dtype), kind="ExternalInput").ap())
    out = nc.dram_tensor("out", laid["x"].shape, F32, kind="ExternalOutput").ap()
    build(nc, *args, out)
    r = run_bass_kernel_spmd(nc, [arrays], core_ids=[0])
    return r.results[0]["out"]
```

```python
import math
from contextlib import ExitStack

import concourse.bass as bass
from concourse import mybir

F32 = mybir.dt.float32
F16 = mybir.dt.float16
I32 = mybir.dt.int32
ALU = mybir.AluOpType
ACT = mybir.ActivationFunctionType
AX_X = mybir.AxisListType.X

P = 128
EPS = 1e-5
X_SCALE = 2.0 ** 10
S_SCALE = 2.0 ** 12
E_LOG = 14 * math.log(2.0)
TOP_EXP = 13


class Arena:

    def __init__(self, tensor, words):
        self.tensor, self.words, self.at = tensor, words, 0

    def take(self, words, dtype=F32, rows=P):
        assert self.at + words <= self.words, (self.at, words, self.words)
        view = self.tensor[0:rows, self.at:self.at + words]
        self.at += words
        return view if dtype == F32 else view.bitcast(dtype)


PASSED = []


def wait_apart(eng, sem, value):
    eng.wait_ge(sem, value)
    eng.sem_inc(PASSED[0], 1)


class Count:

    def __init__(self, eng, sem):
        self.eng, self.sem, self.base, self.n = eng, sem, 0, 0

    def add(self, ins):
        ins.then_inc(self.sem, 1)
        self.n += 1
        return ins

    def wait(self):
        self.eng.wait_ge(self.sem, self.base + self.n)

    def wait_apart(self):
        wait_apart(self.eng, self.sem, self.base + self.n)

    def enter(self, i, per):
        self.outer = (self.base, self.n, per)
        self.base, self.n = self.base + self.n + i * per, 0

    def leave(self, turns):
        base, n, per = self.outer
        assert self.n == per, (self.n, per)
        self.base, self.n = base + n + turns * per, 0


def build(nc, x, norm_w, norm_b, qkv_w, qkv_b, proj_wT, proj_b, phi, ffn_w, ffn_bT, out):
    B, T, C = x.shape
    N, D, _ = ffn_w.shape
    NP = phi.shape[1] * phi.shape[2]
    Q = phi.shape[2]
    NJ = T // P
    K = C // P
    KS = 3 * K
    NB = NP // 512
    NT = NP // P
    TB = 512 // P
    EP = P // Q
    GJ = 4
    XG = B * NJ // GJ
    NG = NJ // GJ
    assert (B, K, TB) == (2, 2, 4)

    x_v = x.rearrange("b (p j) c -> p b j c", j=NJ)
    out_v = out.rearrange("b (p j) c -> p b j c", j=NJ)
    phi_v = phi.rearrange("(k p) n q -> p k (n q)", p=P)
    w_v = ffn_w.rearrange("(t n) (k p) e -> t p n k e", n=EP, p=P)
    d_dram = nc.dram_tensor("logit_difference", [NJ, P, NP], F32, kind="Internal").ap()

    with ExitStack() as ctx:
        def sb(name, shape, dt=F32):
            return ctx.enter_context(nc.sbuf_tensor(name, shape, dt))

        def sem(name):
            return ctx.enter_context(nc.semaphore(name))

        xres = sb("xres", [P, B, NJ, C])
        phs = sb("phs", [P, 2, K, NP], F16)
        xT1 = sb("xT1", [P, 2, K, T], F16)
        ident = sb("ident", [P, P])
        ones = sb("ones", [1, P])
        tcount = sb("tcount", [1, 1])
        epst = sb("epst", [P, 4])
        A_sb = sb("A_sb", [P, B, K, C])
        abc = sb("abc", [P, B, C])
        bT = sb("bT", [P, K, N])
        stat = sb("stat", [P, 2, 8, 6])
        small = sb("small", [P, 480])
        r_xdT = sb("r_xdT", [P, K * T])
        r_xn = sb("r_xn", [P, B * NJ * C])
        r_y = sb("r_y", [P, B * NT * C])
        r_1 = sb("r_1", [P, 6144])
        r_2 = sb("r_2", [P, 4096 + 2048 + 512])

        xdT = r_xdT[:, :].bitcast(F16).rearrange("p (h k t) -> p h k t", h=2, k=K)
        x3n = r_xn[:, :].bitcast(F16).rearrange("p (b j h c) -> p b j h c", b=B, j=NJ, h=2)
        yhl = r_xn[:, :].bitcast(F16).rearrange("p (b t h c) -> p b t h c", b=B, t=NT, h=2)
        yf = r_y[:, :].rearrange("p (b t c) -> p b t c", b=B, t=NT)

        a = Arena(r_xn, B * NJ * C)
        w_raw = a.take(KS * C).rearrange("p (s c) -> p s c", s=KS)
        w_aug = a.take(KS * (C + 1)).rearrange("p (s c) -> p s c", s=KS)
        wbc = a.take(C)
        bbc = a.take(C)
        wpT = a.take(K * C).rearrange("p (k c) -> p k c", k=K)
        G = a.take(K * (C + 1)).rearrange("p (k c) -> p k c", k=K)
        g_row = a.take(C + 1, rows=1)
        u_row = a.take(C, rows=1)
        r_row = a.take(B * C, rows=1)
        c_row = a.take(B * C, rows=1)
        a_row = a.take(B * C, rows=1)
        pb_row = a.take(C, rows=1)
        a = Arena(r_y, B * NT * C)
        x1a = a.take(2 * GJ * B * C).rearrange("p (w j b c) -> p w j b c", w=2, j=GJ, b=B)
        at = a.at
        yb = a.take(GJ * B * C).rearrange("p (j b c) -> p j b c", j=GJ, b=B)
        x3f = a.take(GJ * B * C).rearrange("p (j b c) -> p j b c", j=GJ, b=B)
        a.at = at
        U = a.take(K * C).rearrange("p (k c) -> p k c", k=K)
        S_sb = a.take(B * K * (C + 1)).rearrange("p (b k c) -> p b k c", b=B, k=K)
        R = a.take(B * K * C).rearrange("p (b k c) -> p b k c", b=B, k=K)
        a = Arena(r_1, 6144)
        phf = a.take(K * NP).rearrange("p (k n) -> p k n", k=K)
        junk = a.take(KS * C).rearrange("p (s c) -> p s c", s=KS)
        a = Arena(r_2, 6656)
        Wt = a.take(4096).rearrange("p (w n k e) -> p w n k e", w=2, n=EP, k=K)
        xT = a.take(1024).rearrange("p (w c) -> p w c", w=2)
        xd = a.take(GJ * C).rearrange("p (j c) -> p j c", j=GJ)
        xbuf = sb("xbuf", [P, 4, C + 1])
        a = Arena(r_1, 6144)
        sF = a.take(2048).rearrange("p (w s n) -> p w s n", w=2, s=B)
        shl = a.take(2048, F16).rearrange("p (w h s n) -> p w h s n", w=2, h=2, s=B)
        dS = a.take(1024).rearrange("p (w n) -> p w n", w=2)
        a = Arena(r_2, 6656)
        a.take(4096)
        slT = a.take(2048).rearrange("p (k n b q) -> p k n b q", k=K, n=TB * EP, b=B)
        yT = a.take(512).rearrange("p (e b n) -> p e b n", e=K, b=B)
        a = Arena(r_1, 6144)
        E1, E0, l0 = a.take(2048), a.take(2048), a.take(2048)
        dB = r_xdT[:, 0:2048]
        a = Arena(r_2, 6656)
        eT = a.take(2048, F16).rearrange("p (w h m) -> p w h m", w=4, h=2)
        c1 = a.take(512).rearrange("p (w c) -> p w c", w=2)
        u = a.take(512).rearrange("p (w c) -> p w c", w=2)
        fo = a.take(512).rearrange("p (w c) -> p w c", w=2)
        fz = a.take(512).rearrange("p (w c) -> p w c", w=2)

        sm = Arena(small, 480)
        bcol, qbc = sm.take(KS), sm.take(KS)
        mvx = sm.take(64).rearrange("p (b j s) -> p b j s", b=B, j=NJ)
        rx = sm.take(96).rearrange("p (s b j) -> p s b j", s=3, b=B)
        mvy = sm.take(16).rearrange("p (i s) -> p i s", s=2)
        mv2 = sm.take(16).rearrange("p (i s) -> p i s", s=2)
        ve = sm.take(16)
        ry = sm.take(8)
        ny = sm.take(2 * NJ)
        r3, n3 = sm.take(8), sm.take(8)
        pm = sm.take(2)
        gm = sm.take(2)
        sg = sm.take(2)
        isg = sm.take(2)
        kap = sm.take(2)
        ymx = sm.take(NT)
        m4 = sm.take(8)
        m1 = sm.take(2)
        ebias = sm.take(2)
        zz = sm.take(4 * NJ).rearrange("p (w j s) -> p w j s", w=2, j=NJ)
        mvC = sm.take(4).rearrange("p (w s) -> p w s", w=2)
        tl = sm.take(16).rearrange("p (w s) -> p w s", w=2)

        psL = ctx.enter_context(nc.psum_tensor("psL", [P, 2048], F32))
        bk = [ctx.enter_context(nc.psum_tensor(f"bk{i}", [P, 512], F32)) for i in range(4)]

        par_loaded, rows_loaded = sem("par_loaded"), sem("rows_loaded")
        x_loaded = [sem(f"x_loaded{g}") for g in range(XG)]
        phi_loaded = sem("phi_loaded")
        W_loaded = [sem(f"W_loaded{i}") for i in range(2)]
        pool_const = sem("pool_const")
        PASSED[:] = [sem("passed")]
        dve_own, pool_own = sem("dve_own"), sem("pool_own")
        waug_ready, wbias_ready = sem("waug_ready"), sem("wbias_ready")
        wprod_done, wprod_evac = sem("wprod_done"), sem("wprod_evac")
        stats_x, rstd_x = sem("stats_x"), sem("rstd_x")
        xh_ready, xh_used = sem("xh_ready"), sem("xh_used")
        S_evac = sem("S_evac")
        crow_done, crow_evac = sem("crow_done"), sem("crow_evac")
        arow_done, arow_evac = sem("arow_done"), sem("arow_evac")
        R_done, R_evac = sem("R_done"), sem("R_evac")
        A_done, A_evac = sem("A_done"), sem("A_evac")
        abc_done, abc_ready = sem("abc_done"), sem("abc_ready")
        gmax_in, gmax_out = sem("gmax_in"), sem("gmax_out")
        phi_split = sem("phi_split")
        hT_done, hT_evac = sem("hT_done"), sem("hT_evac")
        y_done, y_read = sem("y_done"), sem("y_read")
        nx_ready, x1_ready, x1a_ready = sem("nx_ready"), sem("x1_ready"), sem("x1a_ready")
        mvy_ready, ry_ready, mv2_ready = sem("mvy_ready"), sem("ry_ready"), sem("mv2_ready")
        r3_ready, x3_ready, x3h_ready, x3l_ready = sem("r3_ready"), sem("x3_ready"), sem("x3h_ready"), sem("x3l_ready")
        xd_ready, x3T_done, x3Th_ready, x3Tl_ready = sem("xd_ready"), sem("x3T_done"), sem("x3Th_ready"), sem("x3Tl_ready")
        d_done, s_ready, d_copied, s_split, slots_used = (
            sem("d_done"), sem("s_ready"), sem("d_copied"), sem("s_split"), sem("slots_used"))
        d_stored = [sem(f"d_stored{i}") for i in range(2)]
        slots_evac = sem("slots_evac")
        yTp_done, yT_ready, yN_done, yN_evac = sem("yTp_done"), sem("yT_ready"), sem("yN_done"), sem("yN_evac")
        yh_ready, yl_ready = sem("yh_ready"), sem("yl_ready")
        l_done, m1_ready, m0_ready, E1_ready, E0_ready = (
            sem("l_done"), sem("m1_ready"), sem("m0_ready"), sem("E1_ready"), sem("E0_ready"))
        eT_done, eTh_ready, eTl_ready, comb_done = (
            sem("eT_done"), sem("eTh_ready"), sem("eTl_ready"), sem("comb_done"))
        c1_ready, u_ready, fin_ready = sem("c1_ready"), sem("u_ready"), sem("fin_ready")
        dB_loaded = sem("dB_loaded")
        out_stored = [sem(f"out_stored{i}") for i in range(2)]

        y_lots = [(b, h) for b in (1, 0) for h in range(NT // 4)]
        YT0 = 2
        N_PAR = 5

        block = ctx.enter_context(nc.Block())

        @block.sync
        def _(sp):
            def load_x(g):
                b, j = g * GJ // NJ, g * GJ % NJ
                sp.dma_start(xres[:, b, j:j + GJ, :], x_v[:, b, j:j + GJ, :]).then_inc(x_loaded[g], 16)

            load_x(0)
            load_x(1)
            sp.dma_start(w_raw, qkv_w.rearrange("(s p) c -> p s c", p=P)).then_inc(par_loaded, 16)
            sp.dma_start(wbc, norm_w.rearrange("(o c) -> o c", o=1).broadcast_to([P, C])).then_inc(par_loaded, 16)
            sp.dma_start(bbc, norm_b.rearrange("(o c) -> o c", o=1).broadcast_to([P, C])).then_inc(par_loaded, 16)
            sp.dma_start(qbc, qkv_b).then_inc(par_loaded, 16)
            sp.dma_start(wpT, proj_wT.rearrange("(k p) e -> p k e", p=P)).then_inc(par_loaded, 16)
            for g in range(2, XG):
                load_x(g)
            sp.dma_start(phf, phi_v).then_inc(phi_loaded, 16)
            for w in range(2):
                sp.dma_start(Wt[:, w], w_v[w]).then_inc(W_loaded[w], 16)

            def block_io(nb, with_y):
                for j in range(NJ):
                    sp.wait_ge(d_copied, nb * NJ + (j + 3))
                    sp.dma_start(d_dram[j, :, bass.ds(nb * 512, 512)], dS[:, j % 2, :]).then_inc(d_stored[j % 2], 16)
                    if with_y and j % 4 == 3:
                        q = j // 4
                        sp.wait_ge(yTp_done, (nb - 1) * TB + (q + 1))
                        sp.dma_start(Wt[:, q % 2], w_v[bass.ds((nb - 1) * TB + (q + 2), 1)].rearrange(
                            "t p n k e -> p (t n) k e")).then_inc(W_loaded[q % 2], 16)

            block_io(0, False)
            with sp.Fori(1, NB) as nb:
                block_io(nb, True)
            for i in range(2):
                sp.wait_ge(d_stored[i], 16 * (NB * NJ // 2 + 1))
            sp.wait_ge(slots_used, NB * NJ + 2)
            sp.dma_start(dB, d_dram[0]).then_inc(dB_loaded, 16)
            for q in range(2):
                sp.wait_ge(yTp_done, (NB - 1) * TB + q + 1)
                sp.dma_start(Wt[:, q % 2], w_v[(NB - 1) * TB + q + 2]).then_inc(W_loaded[q % 2], 16)


            def store(b, j, fin):
                wait_apart(sp, fin_ready, fin + 2)
                w = 1 - b
                sp.dma_start(out_v[:, b, bass.ds(j, 1), :].rearrange("p j c -> p (j c)"),
                             fo[:, w, :]).then_inc(out_stored[w], 16)

            with sp.Fori(0, NJ - 1) as j:
                sp.wait_ge(m0_ready, j + 1)
                sp.dma_start(dB, d_dram[bass.ds(j + 1, 1)].rearrange("j p n -> p (j n)")).then_inc(dB_loaded, 16)
                store(1, j, 2 * j + 1)
                store(0, j, 2 * j + 2)
            store(1, NJ - 1, 2 * NJ - 1)
            store(0, NJ - 1, 2 * NJ)
            for i in range(2):
                sp.wait_ge(out_stored[i], 16 * (NJ + 1))

        @block.gpsimd
        def _(pool):
            own = Count(pool, pool_own)
            pool.sem_inc(fin_ready, 2)
            own.add(nc.gpsimd.memset(ident[:, :], 0.0))
            own.add(nc.gpsimd.memset(epst[:, 0:2], -0.5))
            own.add(nc.gpsimd.memset(epst[:, 2:3], -1.0))
            own.add(nc.gpsimd.memset(ones[:, :], 1.0))
            own.add(nc.gpsimd.memset(tcount[:, :], float(T)))
            own.wait()
            nc.gpsimd.affine_select(out=ident[:, :], in_=ident[:, :], compare_op=ALU.not_equal, fill=1.0,
                                    base=0, pattern=[[-1, P]], channel_multiplier=1).then_inc(pool_const, 1)

            def rsqrt(o, v):
                n = v.shape[1]
                return nc.gpsimd.tensor_tensor(o, v, epst[:, 0:1].broadcast_to([P, n]), ALU.pow)

            for g in range(XG):
                b, j = g * GJ // NJ, g * GJ % NJ
                v = mvx[:, b, j:j + GJ, 1]
                e1 = ve[:, g % 2 * GJ:g % 2 * GJ + GJ]
                e2 = ve[:, 8:8 + GJ]
                pool.wait_ge(stats_x, g + 1)
                own.add(nc.gpsimd.tensor_scalar(e1, v, EPS, 1.0, ALU.add, ALU.mult))
                own.wait()
                own.add(nc.gpsimd.tensor_scalar(e2, e1, EPS, 0.0, ALU.mult, ALU.add))
                own.wait()
                own.add(nc.gpsimd.tensor_tensor(e2, e2, v, ALU.add))
                own.wait()
                rsqrt(rx[:, 1, b, j:j + GJ], e2).then_inc(rstd_x, 1)
                if g % 2 == 1:
                    t8 = slice(j - GJ, j + GJ)
                    own.add(rsqrt(rx[:, 0, b, t8], ve[:, 0:8]))
                    own.wait()
                    own.add(nc.gpsimd.tensor_tensor(rx[:, 2, b, t8], mvx[:, b, t8, 0], rx[:, 0, b, t8], ALU.mult))
                    own.wait()
                    nc.gpsimd.tensor_scalar(rx[:, 2, b, t8], rx[:, 2, b, t8], -1.0, 0.0,
                                            ALU.mult, ALU.add).then_inc(nx_ready, 1)
                if g == 1:
                    pool.wait_ge(par_loaded, 16 * N_PAR)
                    nc.gpsimd.tensor_tensor(w_aug[:, :, 0:C], w_raw, wbc.unsqueeze(1).broadcast_to([P, KS, C]),
                                            ALU.mult).then_inc(waug_ready, 1)
                pool.wait_ge(rstd_x, g + 1)
            pool.wait_ge(gmax_in, 1)
            nc.gpsimd.partition_all_reduce(gm[:, 0:1], pm[:, 0:1], P, bass.bass_isa.ReduceOp.max).then_inc(gmax_out, 1)

            def bias_row(g):
                pool.wait_ge(x1_ready, g + 1)
                for b in range(B):
                    if g == 0:
                        pool.wait_ge(abc_ready, b + 1)
                    ins = nc.gpsimd.tensor_tensor(x1a[:, g % 2, :, b, :], x1a[:, g % 2, :, b, :],
                                                  abc[:, b:b + 1, :].broadcast_to([P, GJ, C]), ALU.add)
                ins.then_inc(x1a_ready, 1)

            def norm_terms(mv, r, n, scale):
                own.wait()
                own.add(nc.gpsimd.tensor_scalar(ve[:, 0:8], mv[:, :, 1], EPS, scale ** -2, ALU.add, ALU.mult))
                own.wait()
                own.add(rsqrt(r, ve[:, 0:8]))
                own.wait()
                own.add(nc.gpsimd.tensor_tensor(n, mv[:, :, 0], r, ALU.mult))
                own.wait()
                return nc.gpsimd.tensor_scalar(n, n, -1.0, 0.0, ALU.mult, ALU.add)

            bias_row(0)
            for p in range(NG + 1):
                gx, gy = p, p - 1
                if gy >= 0:
                    pool.wait_ge(mv2_ready, gy + 1)
                    norm_terms(mv2, r3, n3, X_SCALE).then_inc(r3_ready, 1)
                if gx + 1 < NG:
                    bias_row(gx + 1)
                if gy >= 0:
                    for half in range(2):
                        t2 = slice(2 * half, 2 * half + 2)
                        pool.wait_ge(x3_ready, 2 * gy + half + 1)
                        nc.gpsimd.tensor_tensor(xd[:, t2], x3f[:, t2, 0, :], x3f[:, t2, 1, :],
                                                ALU.subtract).then_inc(xd_ready, 1)
                if gx < NG:
                    pool.wait_ge(mvy_ready, gx + 1)
                    norm_terms(mvy, ry, ny[:, 8 * gx:8 * gx + 8], 1.0).then_inc(ry_ready, 1)
                if gy >= 0:
                    pool.wait_ge(x3h_ready, gy + 1)
                    t4 = slice(gy * GJ, gy * GJ + GJ)
                    for b in range(B):
                        ins = nc.gpsimd.tensor_tensor(x3n[:, b, t4, 1, :], x3f[:, :, b, :], x3n[:, b, t4, 0, :],
                                                      ALU.subtract)
                    ins.then_inc(x3l_ready, 1)

            pool.wait_ge(gmax_in, 2)
            nc.gpsimd.partition_all_reduce(gm[:, 1:2], pm[:, 1:2], P, bass.bass_isa.ReduceOp.max).then_inc(gmax_out, 1)
            pool.wait_ge(gmax_in, 3)

            def finish(b, j, seq, n):
                w = 1 - b
                t = tl[:, w, :]
                pool.wait_ge(u_ready, seq + 3)
                own.add(nc.gpsimd.tensor_tensor(t[:, 0:1], zz[:, w, bass.ds(j, 1), 0], zz[:, w, bass.ds(j, 1), 1], ALU.add))
                own.wait()
                own.add(nc.gpsimd.tensor_tensor(t[:, 1:2], t[:, 0:1], epst[:, 2:3], ALU.pow))
                own.wait()
                own.add(nc.gpsimd.tensor_tensor(t[:, 2:3], t[:, 1:2], isg[:, 1:2], ALU.mult))
                own.wait()
                own.add(nc.gpsimd.tensor_tensor(t[:, 3:4], t[:, 2:3], mvC[:, w, 1:2], ALU.mult))
                own.wait()
                own.add(nc.gpsimd.tensor_tensor(t[:, 3:4], t[:, 3:4], t[:, 2:3], ALU.mult))
                own.wait_apart()
                own.add(nc.gpsimd.tensor_scalar(t[:, 3:4], t[:, 3:4], EPS, 1.0, ALU.add, ALU.mult))
                own.wait()
                own.add(rsqrt(t[:, 4:5], t[:, 3:4]))
                own.wait()
                own.add(nc.gpsimd.tensor_tensor(t[:, 5:6], t[:, 4:5], t[:, 2:3], ALU.mult))
                own.wait()
                own.add(nc.gpsimd.tensor_tensor(t[:, 6:7], t[:, 5:6], mvC[:, w, 0:1], ALU.mult))
                own.wait()
                own.add(nc.gpsimd.tensor_tensor(t[:, 7:8], ny[:, bass.ds(2 * j + b, 1)], t[:, 6:7], ALU.subtract))
                own.wait_apart()
                own.add(nc.gpsimd.tensor_scalar(fz[:, w, :], u[:, w, :], t[:, 5:6], t[:, 7:8], ALU.mult, ALU.add))
                own.wait()
                wait_apart(pool, out_stored[w], 16 * n + 16)
                nc.gpsimd.tensor_tensor(fo[:, w, :], fz[:, w, :],
                                        xres[:, b, bass.ds(j, 1), :].rearrange("p j c -> p (j c)"),
                                        ALU.add).then_inc(fin_ready, 1)

            finish(1, 0, 0, 0)
            with pool.Fori(1, NJ) as j:
                own.enter(j - 1, 22)
                finish(0, j - 1, 2 * j - 1, j - 1)
                finish(1, j, 2 * j, j)
                own.leave(NJ - 1)
            finish(0, NJ - 1, 2 * NJ - 1, NJ - 1)

        @block.scalar
        def _(act):
            act.dma_start(pb_row, proj_b.rearrange("(o c) -> o c", o=1)).then_inc(rows_loaded, 16)
            act.dma_start(bT[:, :, :], ffn_bT.rearrange("(k p) n -> p k n", p=P)).then_inc(rows_loaded, 16)
            act.sem_inc(d_copied, 2)

            def copy(o, i, scale=1.0):
                return nc.scalar.activation(o, i, ACT.Copy, scale=scale)

            act.wait_ge(wprod_done, 1)
            copy(G[:, 0, :], bk[0][:, 0:C + 1]).then_inc(wprod_evac, 1)
            copy(G[:, 1, :], bk[1][:, 0:C + 1]).then_inc(wprod_evac, 1)
            copy(U, bk[2][:, :].rearrange("p (k c) -> p k c", k=K)).then_inc(wprod_evac, 1)
            copy(g_row, bk[3][0:1, 0:C + 1]).then_inc(wprod_evac, 1)
            copy(u_row, psL[0:1, 1536:1536 + C]).then_inc(wprod_evac, 1)
            def x1(g, half):
                if half == 0:
                    act.wait_ge(nx_ready, 3 + g // 2)
                    if g >= 2:
                        act.wait_ge(y_read, GJ * (g - 1))
                for jj in (2 * half, 2 * half + 1):
                    for b in range(B):
                        t = g * GJ + jj
                        ins = nc.scalar.activation(x1a[:, g % 2, jj, b, :], xres[:, b, t, :], ACT.Identity,
                                                   bias=rx[:, 2, b, t:t + 1], scale=rx[:, 0, b, t:t + 1])
                if half == 1:
                    ins.then_inc(x1_ready, 1)

            for b in range(B):
                act.wait_ge(xh_used, NJ * (b + 1))
                copy(S_sb[:, b, 0, :], psL[:, 2 * b * 512:2 * b * 512 + C + 1]).then_inc(S_evac, 1)
                copy(S_sb[:, b, 1, P:], psL[:, (2 * b + 1) * 512:(2 * b + 1) * 512 + P + 1]).then_inc(S_evac, 1)
                act.wait_ge(crow_done, b + 1)
                copy(S_sb[:, b, 1, 0:P], bk[2][:, b * P:(b + 1) * P]).then_inc(crow_evac, 1)
                copy(c_row[:, b * C:(b + 1) * C], bk[3][0:1, b * C:(b + 1) * C]).then_inc(crow_evac, 1)
                act.wait_ge(R_done, b + 1)
                copy(R[:, b], bk[0][:, :].rearrange("p (k c) -> p k c", k=K)).then_inc(R_evac, 1)
                copy(r_row[:, b * C:(b + 1) * C], bk[1][0:1, b * C:(b + 1) * C]).then_inc(R_evac, 1)
                act.wait_ge(arow_done, b + 1)
                arow = psL[0:1, 1024:1024 + C] if b else bk[2][0:1, C:2 * C]
                copy(a_row[:, b * C:(b + 1) * C], arow, scale=1.0 / math.sqrt(C)).then_inc(arow_evac, 1)
                act.wait_ge(A_done, b + 1)
                copy(A_sb[:, b], psL[:, b * 512:(b + 1) * 512].rearrange("p (k c) -> p k c", k=K),
                     scale=1.0 / math.sqrt(C)).then_inc(A_evac, 1)
                act.wait_ge(abc_done, b + 1)
                copy(abc[:, b, :], bk[1][:, b * C:(b + 1) * C]).then_inc(abc_ready, 1)
                if b == 0:
                    x1(0, 0)
                    x1(0, 1)

            def dispatch(nb, j):
                act.wait_ge(d_done, nb * NJ + (j + 1))
                act.wait_ge(s_split, nb * NJ + (j + 1))
                for s in range(B):
                    ins = nc.scalar.activation(sF[:, j % 2, s, :], bk[j % 2][:, :], ACT.Sigmoid, scale=kap[:, s:s + 1])
                ins.then_inc(s_ready, 1)
                act.wait_ge(d_stored[j % 2], nb * (8 * NJ) + (16 * (j // 2) + 16))
                copy(dS[:, j % 2, :], bk[j % 2][:, :]).then_inc(d_copied, 1)

            def block_act(nb):
                for j in range(NJ):
                    dispatch(nb, j)
                    if j % 4 == 0 and j > 0:
                        y_evac(nb - 1, j // 4 - 1)
                y_evac(nb - 1, 3)

            def y_evac(yb_, q):
                act.wait_ge(yN_done, yb_ * TB + (q + 2))
                copy(yf[:, :, bass.ds(yb_ * TB + q, 1), :].rearrange("p b t c -> p b (t c)"),
                     bk[3][:, :].rearrange("p (b c) -> p b c", b=B)).then_inc(yN_evac, 1)

            def xT_evac(t):
                act.wait_ge(hT_done, t + 1)
                if t >= 2:
                    act.wait_ge(y_done, t - 1)
                copy(xT[:, t % 2, :], bk[0 if t < 2 * GJ and t % 2 else 2][:, :]).then_inc(hT_evac, 1)

            def x3_hiT(t):
                act.wait_ge(x3T_done, t + 1)
                pv = bk[2 + t % 2][:, :].rearrange("p (w k t) -> p w k t", w=2, k=K)
                copy(xT1[:, 0, :, t * P:(t + 1) * P], pv[:, 0])
                copy(xdT[:, 0, :, t * P:(t + 1) * P], pv[:, 1]).then_inc(x3Th_ready, 1)

            def x3_float(g, half):
                if half == 0:
                    act.wait_ge(r3_ready, g + 1)
                    if g:
                        act.wait_ge(x3T_done, g * GJ)
                        act.wait_ge(x3l_ready, g)
                for i in range(4 * half, 4 * half + 4):
                    ins = nc.scalar.activation(x3f[:, i // 2, i % 2, :], xres[:, i % 2, g * GJ + i // 2, :], ACT.Identity,
                                               bias=n3[:, i:i + 1], scale=r3[:, i:i + 1])
                ins.then_inc(x3_ready, 1)

            def x3_hi(g):
                act.wait_ge(x3_ready, 2 * g + 2)
                for b in range(B):
                    ins = copy(x3n[:, b, g * GJ:(g + 1) * GJ, 0, :], x3f[:, :, b, :])
                ins.then_inc(x3h_ready, 1)

            for p in range(NG + 2):
                gx, gy, gz = p, p - 1, p - 2
                X, Y, Z = gx < NG, 0 <= gy < NG, gz >= 0
                tx, ty, tz = gx * GJ, gy * GJ, gz * GJ
                if not Z:
                    xT_evac(tx)
                    xT_evac(tx + 1)
                    if gx + 1 < NG:
                        x1(gx + 1, 0)
                    xT_evac(tx + 2)
                    if gx + 1 < NG:
                        x1(gx + 1, 1)
                    xT_evac(tx + 3)
                    if Y:
                        x3_float(gy, 0)
                        x3_float(gy, 1)
                        x3_hiT(ty)
                        x3_hiT(ty + 1)
                        x3_hi(gy)
                        x3_hiT(ty + 2)
                        x3_hiT(ty + 3)
                else:
                    if Z:
                        if gz == 0:
                            act.wait_ge(phi_split, 1)
                        dispatch(0, tz)
                    if X:
                        xT_evac(tx)
                    if Z:
                        dispatch(0, tz + 1)
                    if X:
                        xT_evac(tx + 1)
                    if gx + 1 < NG:
                        x1(gx + 1, 0)
                    if X:
                        xT_evac(tx + 2)
                    if Z:
                        dispatch(0, tz + 2)
                    if gx + 1 < NG:
                        x1(gx + 1, 1)
                    if X:
                        xT_evac(tx + 3)
                    if Z:
                        dispatch(0, tz + 3)
                    if Y:
                        x3_float(gy, 0)
                        x3_float(gy, 1)
                        x3_hiT(ty)
                        x3_hiT(ty + 1)
                        x3_hi(gy)
                        x3_hiT(ty + 2)
                        x3_hiT(ty + 3)

            with act.Fori(1, NB) as nb:
                block_act(nb)
            def y_hi(i):
                b, h = y_lots[i]
                t4 = slice(4 * h, 4 * h + 4)
                nc.scalar.activation(yhl[:, b, t4, 0, :], yf[:, b, t4, :], ACT.Identity,
                                     scale=sg[:, 1:2]).then_inc(yh_ready, 1)

            def hi(m, gq):
                act.wait_ge(eT_done, m + 1)
                act.wait_ge(comb_done, m + 1)
                copy(eT[:, gq, 0, :], bk[gq % 2][:, :]).then_inc(eTh_ready, 1)

            def expo(b, j, half):
                src, dst = (psL, E1) if b else (l0, E0)
                w = 1 - b
                nc.scalar.activation(dst[:, 1024 * half:1024 * half + 1024], src[:, 1024 * half:1024 * half + 1024],
                                     ACT.Exp, bias=ebias[:, w:w + 1], scale=kap[:, 0:1],
                                     accum_out=zz[:, w, bass.ds(j, 1), half]).then_inc(
                                         E1_ready if b else E0_ready, 1)

            def c1_copy(b, seq, m_end):
                act.wait_ge(comb_done, m_end + 4)
                act.wait_ge(u_ready, seq + 1)
                copy(c1[:, 1 - b, :], bk[3 - b][:, 256:512]).then_inc(c1_ready, 1)

            def batch1_act(j):
                hi(8 * j, 0)
                hi(8 * j + 1, 1)
                act.wait_ge(m0_ready, j + 1)
                expo(0, j, 0)
                hi(8 * j + 2, 2)
                expo(0, j, 1)
                c1_copy(0, 2 * j - 1, 8 * j)
                hi(8 * j + 3, 3)

            def comb_act(j):
                hi(8 * j - 4, 0)
                hi(8 * j - 3, 1)
                c1_copy(1, 2 * j - 2, 8 * j - 4)
                hi(8 * j - 2, 2)
                act.wait_ge(m1_ready, j + 1)
                expo(1, j, 0)
                hi(8 * j - 1, 3)
                expo(1, j, 1)
                batch1_act(j)

            act.wait_ge(slots_used, NB * NJ + 2)
            y_evac(NB - 1, 0)
            y_evac(NB - 1, 1)
            act.wait_ge(m1_ready, 1)
            expo(1, 0, 0)
            expo(1, 0, 1)
            y_evac(NB - 1, 2)
            hi(0, 0)
            act.wait_ge(m0_ready, 1)
            expo(0, 0, 0)
            y_evac(NB - 1, 3)
            expo(0, 0, 1)
            hi(1, 1)
            act.wait_ge(gmax_in, 3)
            act.wait_ge(yN_evac, NB * TB + 1)
            y_hi(0)
            y_hi(1)
            y_hi(2)
            hi(2, 2)
            y_hi(3)
            hi(3, 3)
            y_hi(4)
            hi(4, 0)
            y_hi(5)
            act.wait_ge(m1_ready, 2)
            expo(1, 1, 0)
            hi(5, 1)
            c1_copy(1, 0, 4)
            y_hi(6)
            hi(6, 2)
            expo(1, 1, 1)
            y_hi(7)
            hi(7, 3)
            batch1_act(1)
            with act.Fori(2, NJ) as j:
                comb_act(j)
            hi(8 * NJ - 4, 0)
            hi(8 * NJ - 3, 1)
            c1_copy(1, 2 * NJ - 2, 8 * NJ - 4)
            hi(8 * NJ - 2, 2)
            hi(8 * NJ - 1, 3)
            c1_copy(0, 2 * NJ - 1, 8 * NJ)

        @block.vector
        def _(dve):
            own = Count(dve, dve_own)
            V = nc.vector
            dve.sem_inc(s_split, 2)
            dve.sem_inc(slots_evac, 4)
            dve.sem_inc(eTl_ready, 2)
            dve.sem_inc(u_ready, 2)
            for i in range(2):
                dve.sem_inc(d_stored[i], 16)
                dve.sem_inc(out_stored[i], 16)

            own.add(V.memset(xbuf[:, :, C:C + 1], 1.0))

            def stats(g):
                b, j = g * GJ // NJ, g * GJ % NJ
                dve.wait_ge(x_loaded[g], 16)
                if g >= 2:
                    dve.wait_ge(stats_x, g - 1)
                for i in range(GJ):
                    own.add(V.bn_stats(stat[:, g % 2, i, :], xres[:, b, j + i, :]))
                own.wait()
                for i in range(GJ):
                    ins = V.bn_aggr(mvx[:, b, j + i, :], stat[:, g % 2, i, :])
                ins.then_inc(stats_x, 1)

            stats(0)
            for g in range(XG):
                if g + 1 < XG:
                    stats(g + 1)
                if g == 1:
                    dve.wait_ge(par_loaded, 16 * N_PAR)
                    for s in range(KS):
                        own.add(V.tensor_tensor_reduce(junk[:, s, :], w_raw[:, s, :], bbc, 1.0, 0.0, ALU.mult, ALU.add,
                                                       bcol[:, s:s + 1]))
                    own.wait()
                    V.tensor_tensor(w_aug[:, :, C], bcol, qbc, ALU.add).then_inc(wbias_ready, 1)
                b, j = g * GJ // NJ, g * GJ % NJ
                dve.wait_ge(rstd_x, g + 1)
                if g == 0:
                    own.wait()
                for i in range(GJ):
                    t = g * GJ + i
                    if t >= 4:
                        dve.wait_ge(xh_used, t - 3)
                    V.tensor_scalar(xbuf[:, t % 4, 0:C], xres[:, b, j + i, :], mvx[:, b, j + i, 0:1],
                                    rx[:, 1, b, j + i:j + i + 1], ALU.subtract, ALU.mult).then_inc(xh_ready, 1)

            def pow2_scale(i):
                c = slice(i, i + 1)
                own.add(V.tensor_scalar(gm[:, c], gm[:, c], 2.0 ** -100, None, ALU.max))
                own.wait()
                own.add(V.tensor_scalar(gm[:, c].bitcast(I32), gm[:, c].bitcast(I32), 0x7F800000, None, ALU.bitwise_and))
                own.wait()
                own.add(V.tensor_scalar(isg[:, c], gm[:, c], 2.0 ** -TOP_EXP, None, ALU.mult))
                own.wait()
                own.add(V.reciprocal(sg[:, c], isg[:, c]))
                own.wait()

            def xhat(t):
                if t >= 2:
                    dve.wait_ge(hT_done, t - 1)
                for b in range(B):
                    ins = V.tensor_scalar(xbuf[:, 2 * (t % 2) + b, 0:C], xres[:, b, t, :],
                                          mvx[:, b, t, 0:1], rx[:, 1, b, t:t + 1], ALU.subtract, ALU.mult)
                ins.then_inc(xh_ready, 1)

            dve.wait_ge(xh_used, B * NJ)
            xhat(0)
            xhat(1)
            dve.wait_ge(phi_loaded, 16)
            V.tensor_reduce(pm[:, 0:1], phf.rearrange("p k n -> p (k n)"), AX_X, ALU.max,
                            apply_absolute_value=True).then_inc(gmax_in, 1)
            dve.wait_ge(gmax_out, 1)
            pow2_scale(0)
            own.add(V.tensor_scalar(kap[:, 0:1], isg[:, 0:1], 1.0 / X_SCALE, None, ALU.mult))
            own.add(V.tensor_scalar(kap[:, 1:2], isg[:, 0:1], -1.0 / X_SCALE, None, ALU.mult))
            own.add(V.tensor_scalar(phs[:, 0], phf, sg[:, 0:1], None, ALU.mult))
            own.wait()
            V.scalar_tensor_tensor(phs[:, 1].rearrange("p k n -> p (k n)"), phf.rearrange("p k n -> p (k n)"),
                                   sg[:, 0:1], phs[:, 0].rearrange("p k n -> p (k n)"), ALU.mult,
                                   ALU.subtract).then_inc(phi_split, 1)

            def attn(t):
                dve.wait_ge(y_done, t + 1)
                if t % GJ == 0:
                    dve.wait_ge(x1a_ready, t // GJ + 1)
                V.tensor_tensor(yb[:, t % GJ], bk[1 if t < 2 * GJ and t % 2 else 3][:, :].rearrange("p (b c) -> p b c", b=B),
                                x1a[:, t // GJ % 2, t % GJ], ALU.add).then_inc(y_read, 1)

            def x3_loT(t):
                dve.wait_ge(x3Th_ready, t + 1)
                pv = bk[2 + t % 2][:, :].rearrange("p (w k t) -> p w k t", w=2, k=K)
                cols = slice(t * P, (t + 1) * P)
                V.tensor_tensor(xT1[:, 1, :, cols], pv[:, 0], xT1[:, 0, :, cols], ALU.subtract)
                V.tensor_tensor(xdT[:, 1, :, cols], pv[:, 1], xdT[:, 0, :, cols], ALU.subtract).then_inc(x3Tl_ready, 1)

            def split(nb, j):
                dve.wait_ge(s_ready, nb * NJ + (j + 1))
                dve.wait_ge(slots_used, nb * NJ + (j + 1))
                own.add(V.tensor_scalar(shl[:, j % 2, 0], sF[:, j % 2], S_SCALE, None, ALU.mult))
                own.wait()
                V.scalar_tensor_tensor(shl[:, j % 2, 1], sF[:, j % 2], S_SCALE, shl[:, j % 2, 0],
                                       ALU.mult, ALU.subtract).then_inc(s_split, 1)

            def residual(g):
                dve.wait_ge(ry_ready, g + 1)
                for i in range(8):
                    t = g * GJ + i // 2
                    own.add(V.scalar_tensor_tensor(xres[:, i % 2, t, :], yb[:, i // 2, i % 2, :], ry[:, i:i + 1],
                                                   xres[:, i % 2, t, :], ALU.mult, ALU.add))
                own.wait()

            def stats_x2(g):
                if g:
                    dve.wait_ge(r3_ready, g)
                for i in range(8):
                    own.add(V.bn_stats(stat[:, 1, i, :], xres[:, i % 2, g * GJ + i // 2, :]))
                own.wait()
                for i in range(8):
                    ins = V.bn_aggr(mv2[:, i, :], stat[:, 1, i, :])
                ins.then_inc(mv2_ready, 1)

            def stats_y(g, half):
                dve.wait_ge(y_read, g * GJ + 2 * half + 2)
                for i in range(4 * half, 4 * half + 4):
                    own.add(V.bn_stats(stat[:, 0, i, :], yb[:, i // 2, i % 2, :]))
                if half == 1:
                    own.wait()
                    for i in range(8):
                        ins = V.bn_aggr(mvy[:, i, :], stat[:, 0, i, :])
                    ins.then_inc(mvy_ready, 1)

            for p in range(NG + 2):
                gx, gy, gz = p, p - 1, p - 2
                X, Y, Z = gx < NG, 0 <= gy < NG, gz >= 0
                tx, ty, tz = gx * GJ, gy * GJ, gz * GJ
                if not Z:
                    if Y:
                        residual(gy)
                    xhat(tx + 2)
                    if Y:
                        stats_x2(gy)
                    xhat(tx + 3)
                    attn(tx)
                    attn(tx + 1)
                    attn(tx + 2)
                    attn(tx + 3)
                    stats_y(gx, 0)
                    stats_y(gx, 1)
                    if Y:
                        x3_loT(ty)
                        x3_loT(ty + 1)
                    if gx + 1 < NG:
                        xhat(tx + GJ)
                        xhat(tx + GJ + 1)
                    if Y:
                        x3_loT(ty + 2)
                        x3_loT(ty + 3)
                else:
                    if Y:
                        residual(gy)
                    if Z:
                        split(0, tz)
                    if X:
                        attn(tx)
                        xhat(tx + 2)
                    if Z:
                        split(0, tz + 1)
                    if Y:
                        stats_x2(gy)
                    if X:
                        attn(tx + 1)
                        xhat(tx + 3)
                        attn(tx + 2)
                    if Z:
                        split(0, tz + 2)
                    if X:
                        stats_y(gx, 0)
                        attn(tx + 3)
                    if Z:
                        split(0, tz + 3)
                    if X:
                        stats_y(gx, 1)
                    if gx + 1 < NG:
                        xhat(tx + GJ)
                        xhat(tx + GJ + 1)
                    if Y:
                        x3_loT(ty)
                        x3_loT(ty + 1)
                        x3_loT(ty + 2)
                        x3_loT(ty + 3)

            def block_dve(nb, last):
                for j in range(1, NJ):
                    split(nb, j)
                    if j % 4 == 2:
                        y_bias(nb - 1, j // 4)
                if not last:
                    split(nb + 1, 0)
                slots_out(nb)

            def slots_out(nb):
                dve.wait_ge(slots_used, nb * NJ + (NJ + 2))
                for k in range(K):
                    for b in range(B):
                        i = k * B + b
                        V.tensor_scalar(slT[:, k, :, b, :],
                                        psL[:, i * 512:(i + 1) * 512].rearrange("p (n q) -> p n q", q=Q),
                                        1.0 / (X_SCALE * S_SCALE), None, ALU.mult).then_inc(slots_evac, 1)

            def y_bias(yb_, q):
                dve.wait_ge(yTp_done, yb_ * TB + (q + 1))
                dve.wait_ge(yN_done, yb_ * TB + (q + 1))
                own.wait()
                for e in range(K):
                    V.tensor_tensor(
                        yT[:, e].rearrange("p b (n q) -> p b n q", q=Q),
                        bk[2][:, e * 256:(e + 1) * 256].rearrange("p (n b q) -> p b n q", n=EP, b=B),
                        bT[:, e, bass.ds((yb_ * TB + q) * EP, EP)].unsqueeze(1).unsqueeze(3).broadcast_to([P, B, EP, Q]),
                        ALU.add).then_inc(yT_ready, 1)
                dve.wait_ge(yT_ready, (yb_ * TB + q) * 2 + 4)
                own.add(V.tensor_reduce(ymx[:, bass.ds(yb_ * TB + q, 1)], yT.rearrange("p e b n -> p (e b n)"),
                                        AX_X, ALU.max, apply_absolute_value=True))

            split(1, 0)
            slots_out(0)
            with dve.Fori(1, NB - 1) as nb:
                own.enter(nb - 1, NJ + TB)
                block_dve(nb, False)
                own.leave(NB - 2)
            block_dve(NB - 1, True)
            def lo(m, gq):
                dve.wait_ge(eTh_ready, m + 1)
                V.tensor_tensor(eT[:, gq, 1, :], bk[gq % 2][:, :], eT[:, gq, 0, :], ALU.subtract).then_inc(eTl_ready, 1)

            def maxima(j, w, last):
                own.wait()
                own.add(V.tensor_reduce(m1[:, w:w + 1], m4[:, 4 * w:4 * w + 4], AX_X, ALU.max))
                own.wait()
                V.tensor_scalar(ebias[:, w:w + 1], m1[:, w:w + 1], kap[:, 1:2], E_LOG, ALU.mult, ALU.add).then_inc(last, 1)

            def add_max(j, kb):
                c = slice(512 * kb, 512 * kb + 512)
                own.add(V.tensor_tensor_reduce(l0[:, c], psL[:, c], dB[:, c], 1.0, -3.0e38, ALU.add, ALU.max,
                                               m4[:, 4 + kb:5 + kb]))

            def tail(b, seq):
                w = 1 - b
                dve.wait_ge(c1_ready, seq + 1)
                own.add(V.tensor_tensor(u[:, w, :], bk[3 - b][:, 0:256], c1[:, w, :], ALU.add))
                own.wait()
                own.add(V.bn_stats(stat[:, 0, w, :], u[:, w, :]))
                own.wait_apart()
                V.bn_aggr(mvC[:, w, :], stat[:, 0, w, :]).then_inc(u_ready, 1)

            def l_max(j, kb):
                dve.wait_ge(l_done, 4 * j + kb + 1)
                own.add(V.tensor_reduce(m4[:, kb:kb + 1], psL[:, 512 * kb:512 * kb + 512], AX_X, ALU.max))

            def differences(j, between):
                dve.wait_ge(E0_ready, 2 * j)
                dve.wait_ge(dB_loaded, 16 * j + 16)
                wait_apart(dve, E1_ready, 2 * j + 1)
                add_max(j, 0)
                add_max(j, 1)
                between()
                wait_apart(dve, E1_ready, 2 * j + 2)
                add_max(j, 2)
                add_max(j, 3)
                maxima(j, 1, m0_ready)
                for gq in range(3):
                    lo(8 * j + gq, gq)
                dve.wait_ge(fin_ready, 2 * j)
                tail(0, 2 * j - 1)
                lo(8 * j + 3, 3)

            def comb_dve(j):
                lo(8 * j - 4, 0)
                lo(8 * j - 3, 1)
                dve.wait_ge(fin_ready, 2 * j - 1)
                tail(1, 2 * j - 2)
                for kb in range(4):
                    l_max(j, kb)
                maxima(j, 0, m1_ready)
                lo(8 * j - 2, 2)
                differences(j, lambda: lo(8 * j - 1, 3))

            def y_lo(i):
                b, h = y_lots[i]
                t4 = slice(4 * h, 4 * h + 4)
                dve.wait_ge(yh_ready, i + 1)
                V.scalar_tensor_tensor(yhl[:, b, t4, 1, :], yf[:, b, t4, :], sg[:, 1:2], yhl[:, b, t4, 0, :],
                                       ALU.mult, ALU.subtract).then_inc(yl_ready, 1)

            l_max(0, 0)
            l_max(0, 1)
            y_bias(NB - 1, 0)
            l_max(0, 2)
            y_bias(NB - 1, 1)
            l_max(0, 3)
            maxima(0, 0, m1_ready)
            y_bias(NB - 1, 2)
            dve.wait_ge(dB_loaded, 16)
            dve.wait_ge(E1_ready, 1)
            add_max(0, 0)
            add_max(0, 1)
            dve.wait_ge(E1_ready, 2)
            add_max(0, 2)
            add_max(0, 3)
            maxima(0, 1, m0_ready)
            y_bias(NB - 1, 3)
            own.wait()
            V.tensor_reduce(pm[:, 1:2], ymx, AX_X, ALU.max).then_inc(gmax_in, 1)
            lo(0, 0)
            dve.wait_ge(gmax_out, 2)
            pow2_scale(1)
            dve.sem_inc(gmax_in, 1)
            lo(1, 1)
            y_lo(0)
            y_lo(1)
            y_lo(2)
            lo(2, 2)
            y_lo(3)
            lo(3, 3)
            l_max(1, 0)
            l_max(1, 1)
            y_lo(4)
            lo(4, 0)
            l_max(1, 2)
            l_max(1, 3)
            maxima(1, 0, m1_ready)
            y_lo(5)
            lo(5, 1)
            tail(1, 0)
            y_lo(6)
            lo(6, 2)
            differences(1, lambda: (y_lo(7), lo(7, 3)))
            with dve.Fori(2, NJ) as j:
                own.enter(j - 2, 10 + 4)
                comb_dve(j)
                own.leave(NJ - 2)
            lo(8 * NJ - 4, 0)
            lo(8 * NJ - 3, 1)
            dve.wait_ge(fin_ready, 2 * NJ - 1)
            tail(1, 2 * NJ - 2)
            lo(8 * NJ - 2, 2)
            lo(8 * NJ - 1, 3)
            dve.wait_ge(fin_ready, 2 * NJ)
            tail(0, 2 * NJ - 1)

        @block.tensor
        def _(pe):
            mm = nc.tensor.matmul
            pe.sem_inc(slots_used, 2)
            pe.sem_inc(comb_done, 4)

            def weight_products():
                pe.wait_ge(waug_ready, 1)
                pe.wait_ge(wbias_ready, 1)
                wq, wk, wv = w_aug[:, 0:K], w_aug[:, K:2 * K], w_aug[:, 2 * K:3 * K]
                for i in range(K):
                    for k in range(K):
                        mm(bk[i][:, 0:C + 1], wk[:, k, i * P:(i + 1) * P], wq[:, k, :], start=(k == 0), stop=(k == K - 1))
                for i in range(K):
                    for k in range(K):
                        mm(bk[2][:, i * C:(i + 1) * C], wv[:, k, i * P:(i + 1) * P], wpT[:, k, :], start=(k == 0), stop=(k == K - 1))
                for k in range(K):
                    mm(bk[3][0:1, 0:C + 1], wk[:, k, C:C + 1], wq[:, k, :], start=(k == 0), stop=(k == K - 1))
                for k in range(K):
                    ins = mm(psL[0:1, 1536:1536 + C], wv[:, k, C:C + 1], wpT[:, k, :], start=(k == 0), stop=(k == K - 1))
                ins.then_inc(wprod_done, 1)

            def s_tile(t):
                b, j = t // NJ, t % NJ
                pe.wait_ge(xh_ready, t + 1)
                for k in range(K):
                    o = (b * K + k) * 512
                    ins = mm(psL[:, o:o + C + 1 - k * P], xbuf[:, t % 4, k * P:(k + 1) * P], xbuf[:, t % 4, k * P:],
                             start=(j == 0), stop=(j == NJ - 1))
                ins.then_inc(xh_used, 1)

            def c_row_step(b):
                pe.wait_ge(S_evac, K * (b + 1))
                nc.tensor.transpose(bk[2][:, b * P:(b + 1) * P], S_sb[:, b, 0, P:C], ident[:, :])
                for k in range(K):
                    ins = mm(bk[3][0:1, b * C + k * P:b * C + (k + 1) * P], S_sb[:, b, k, C:C + 1], ident[:, :],
                             start=True, stop=True)
                ins.then_inc(crow_done, 1)

            def R_step(b):
                if b:
                    pe.wait_ge(R_evac, 2)
                for k in range(K):
                    mm(bk[1][0:1, b * C:(b + 1) * C], S_sb[:, b, k, C:C + 1], U[:, k, :], start=(k == 0), stop=False)
                mm(bk[1][0:1, b * C:(b + 1) * C], tcount[:, :], u_row, start=False, stop=True)
                pe.wait_ge(crow_evac, 2 * (b + 1))
                for i in range(K):
                    for k in range(K):
                        mm(bk[0][:, i * C:(i + 1) * C], S_sb[:, b, k, i * P:(i + 1) * P], U[:, k, :], start=(k == 0), stop=False)
                    ins = mm(bk[0][:, i * C:(i + 1) * C], c_row[:, b * C + i * P:b * C + (i + 1) * P], u_row, start=False, stop=True)
                ins.then_inc(R_done, 1)

            def A_step(b):
                pe.wait_ge(R_evac, 2 * (b + 1))
                arow = psL[0:1, 1024:1024 + C] if b else bk[2][0:1, C:2 * C]
                for k in range(K):
                    mm(arow, G[:, k, C:C + 1], R[:, b, k, :], start=(k == 0), stop=False)
                mm(arow, g_row[:, C:C + 1], r_row[:, b * C:(b + 1) * C], start=False, stop=True).then_inc(arow_done, 1)
                for i in range(K):
                    o = b * 512 + i * C
                    for k in range(K):
                        mm(psL[:, o:o + C], G[:, k, i * P:(i + 1) * P], R[:, b, k, :], start=(k == 0), stop=False)
                    ins = mm(psL[:, o:o + C], g_row[:, i * P:(i + 1) * P], r_row[:, b * C:(b + 1) * C], start=False, stop=True)
                ins.then_inc(A_done, 1)

            def abc_step(b):
                if b == 0:
                    pe.wait_ge(rows_loaded, 32)
                pe.wait_ge(arow_evac, b + 1)
                mm(bk[1][:, b * C:(b + 1) * C], ones[:, :], a_row[:, b * C:(b + 1) * C], start=True, stop=False)
                mm(bk[1][:, b * C:(b + 1) * C], ones[:, :], pb_row, start=False, stop=True).then_inc(abc_done, 1)

            for t in range(B * NJ):
                if t == 3 * GJ:
                    weight_products()
                if t == NJ:
                    pe.wait_ge(pool_const, 1)
                    pe.wait_ge(wprod_evac, 5)
                s_tile(t)
                if t == NJ + 2:
                    c_row_step(0)
                if t == NJ + 4:
                    R_step(0)
                if t == NJ + 7:
                    A_step(0)
                if t == NJ + 8:
                    abc_step(0)
            c_row_step(1)
            R_step(1)
            A_step(1)
            abc_step(1)
            pe.wait_ge(A_evac, 2)

            def h_banks(t):
                return (bk[0], bk[1]) if t < 2 * GJ and t % 2 else (bk[2], bk[3])

            def h_transpose(t):
                pe.wait_ge(xh_ready, B * NJ + t + 1)
                if t < 2 * GJ:
                    if t >= 2:
                        pe.wait_ge(hT_evac, t - 1)
                else:
                    pe.wait_ge(hT_evac, t)
                if t % GJ == 0 and t >= 2 * GJ:
                    pe.wait_ge(x3Tl_ready, t - 2 * GJ + 3)
                for b in range(B):
                    for k in range(K):
                        i = b * K + k
                        ins = nc.tensor.transpose(h_banks(t)[0][:, i * P:(i + 1) * P],
                                                  xbuf[:, 2 * (t % 2) + b, k * P:(k + 1) * P], ident[:, :])
                ins.then_inc(hT_done, 1)

            def h_product(t):
                pe.wait_ge(hT_evac, t + 1)
                if t == 1:
                    pe.wait_ge(abc_ready, 2)
                if t < 2 * GJ:
                    if t >= 2:
                        pe.wait_ge(y_read, t - 1)
                else:
                    pe.wait_ge(y_read, t)
                if t % GJ == 0 and t >= 2 * GJ:
                    pe.wait_ge(x3Tl_ready, t - 2 * GJ + 4)
                for b in range(B):
                    for k in range(K):
                        i = b * K + k
                        ins = mm(h_banks(t)[1][:, b * C:(b + 1) * C], xT[:, t % 2, i * P:(i + 1) * P],
                                 A_sb[:, b, k, :], start=(k == 0), stop=(k == K - 1))
                ins.then_inc(y_done, 1)

            def x3_transpose(t):
                jj = t % GJ
                if jj % 2 == 0:
                    pe.wait_ge(xd_ready, t // 2 + 1)
                if jj == 0:
                    pe.wait_ge(hT_evac, min(NJ, t + 2 * GJ))
                if jj == 1:
                    pe.wait_ge(y_read, min(NJ, t - 1 + 2 * GJ))
                if t >= 2:
                    pe.wait_ge(x3Tl_ready, t - 1)
                for w in range(2):
                    for k in range(K):
                        src = xd[:, jj, k * P:(k + 1) * P] if w else x3f[:, jj, 1, k * P:(k + 1) * P]
                        o = (w * K + k) * P
                        ins = nc.tensor.transpose(bk[2 + t % 2][:, o:o + P], src, ident[:, :])
                ins.then_inc(x3T_done, 1)

            def d_tile(nb, j):
                pe.wait_ge(d_copied, nb * NJ + (j + 1))
                for k in range(K):
                    for hx, hp in ((0, 0), (0, 1), (1, 0)):
                        ins = mm(bk[j % 2][:, :], xdT[:, hx, k, j * P:(j + 1) * P], phs[:, hp, k, bass.ds(nb * 512, 512)],
                                 start=(k == 0 and hx + hp == 0), stop=(k == K - 1 and hx == 1))
                ins.then_inc(d_done, 1)

            def slots(nb, j):
                pe.wait_ge(s_split, nb * NJ + (j + 3))
                for k in range(K):
                    for b in range(B):
                        i = k * B + b
                        if j == 0:
                            pe.wait_ge(slots_evac, nb * 4 + (i + 1))
                        for hx, hs in ((0, 0), (0, 1), (1, 0)):
                            ins = mm(psL[:, i * 512:(i + 1) * 512], x3n[:, b, j, hx, k * P:(k + 1) * P],
                                     shl[:, j % 2, hs, b, :], start=(j == 0 and hx + hs == 0), stop=(j == NJ - 1 and hx == 1))
                ins.then_inc(slots_used, 1)

            def y_product(yb_, q):
                pe.wait_ge(W_loaded[q % 2], yb_ * (8 * TB) + (16 * (q // 2) + 16))
                if q == 0:
                    pe.wait_ge(slots_evac, yb_ * 4 + 8)
                pe.wait_ge(yT_ready, (yb_ * TB + q) * 2 + YT0)
                for n in range(EP):
                    for e in range(K):
                        for k in range(K):
                            o = e * 256 + n * 64
                            ins = mm(bk[2][:, o:o + 64], Wt[:, q % 2, n, k, e * P:(e + 1) * P],
                                     slT[:, k, q * EP + n].rearrange("p b q -> p (b q)"), start=(k == 0), stop=(k == K - 1))
                ins.then_inc(yTp_done, 1)

            def y_turn(yb_, q):
                pe.wait_ge(yT_ready, (yb_ * TB + q) * 2 + YT0 + 2)
                pe.wait_ge(yN_evac, yb_ * TB + q + 1)
                for b in range(B):
                    for e in range(K):
                        o = b * 256 + e * P
                        ins = nc.tensor.transpose(bk[3][:, o:o + P], yT[:, e, b, :], ident[:, :])
                ins.then_inc(yN_done, 1)

            pe.sem_inc(yT_ready, YT0)
            pe.sem_inc(yN_evac, 1)
            pe.sem_inc(yN_done, 1)

            for p in range(NG + 2):
                gx, gy, gz = p, p - 1, p - 2
                X, Y, Z = gx < NG, 0 <= gy < NG, gz >= 0
                tx, ty, tz = gx * GJ, gy * GJ, gz * GJ
                if not Z:
                    h_transpose(tx)
                    h_transpose(tx + 1)
                    h_product(tx)
                    h_transpose(tx + 2)
                    h_product(tx + 1)
                    h_transpose(tx + 3)
                    h_product(tx + 2)
                    h_product(tx + 3)
                    if Y:
                        x3_transpose(ty)
                        x3_transpose(ty + 1)
                        x3_transpose(ty + 2)
                        x3_transpose(ty + 3)
                else:
                    if Z:
                        if gz == 0:
                            pe.wait_ge(phi_split, 1)
                        pe.wait_ge(x3Tl_ready, tz + 1)
                        d_tile(0, tz)
                    if X:
                        h_transpose(tx)
                    if Z:
                        pe.wait_ge(x3Tl_ready, tz + 2)
                        d_tile(0, tz + 1)
                    if X:
                        h_product(tx)
                        h_transpose(tx + 1)
                    if Z:
                        pe.wait_ge(x3l_ready, gz + 1)
                        slots(0, tz)
                    if X:
                        h_product(tx + 1)
                        h_transpose(tx + 2)
                    if Z:
                        pe.wait_ge(x3Tl_ready, tz + 3)
                        d_tile(0, tz + 2)
                        slots(0, tz + 1)
                    if X:
                        h_product(tx + 2)
                        h_transpose(tx + 3)
                    if Z:
                        pe.wait_ge(x3Tl_ready, tz + 4)
                        d_tile(0, tz + 3)
                    if X:
                        h_product(tx + 3)
                    if Z:
                        slots(0, tz + 2)
                        if gz == NG - 1:
                            d_tile(1, 0)
                        slots(0, tz + 3)
                        if gz == NG - 1:
                            d_tile(1, 1)
                    if Y:
                        x3_transpose(ty)
                        x3_transpose(ty + 1)
                        x3_transpose(ty + 2)
                        x3_transpose(ty + 3)

            def slots_ahead(nb, j, last):
                slots(nb, j)
                if j + 2 < NJ:
                    d_tile(nb, j + 2)
                elif not last:
                    d_tile(nb + 1, j + 2 - NJ)

            def block_pe(nb, last):
                for j in range(NJ):
                    slots_ahead(nb, j, last)
                    if j % 4 == 1:
                        y_product(nb - 1, j // 4)
                    if j % 4 == 2:
                        y_turn(nb - 1, j // 4)

            with pe.Fori(1, NB - 1) as nb:
                block_pe(nb, False)
            block_pe(NB - 1, True)

            def logits(j, kbs):
                for kb in kbs:
                    for k in range(K):
                        for hx, hp in ((0, 0), (0, 1), (1, 0)):
                            ins = mm(psL[:, kb * 512:(kb + 1) * 512], xT1[:, hx, k, bass.ds(j * P, P)],
                                     phs[:, hp, k, kb * 512:(kb + 1) * 512],
                                     start=(k == 0 and hx + hp == 0), stop=(k == K - 1 and hx == 1))
                    ins.then_inc(l_done, 1)

            def turn(b, j, m, gq):
                pe.wait_ge(E1_ready if b else E0_ready, 2 * j + 1 + gq // 2)
                pe.wait_ge(eTl_ready, m + 1)
                E = E1 if b else E0
                for i in range(4):
                    o = gq * 512 + i * P
                    ins = nc.tensor.transpose(bk[gq % 2][:, i * P:(i + 1) * P], E[:, o:o + P], ident[:, :])
                ins.then_inc(eT_done, 1)

            def high(b, seq, m, gq):
                pe.wait_ge(eTh_ready, m + 1)
                if gq == 0:
                    pe.wait_ge(u_ready, seq + 1)
                for i in range(4):
                    t = gq * 4 + i
                    mm(bk[3 - b][:, :], eT[:, gq, 0, i * P:(i + 1) * P], yhl[:, b, t].rearrange("p h c -> p (h c)"),
                       start=(t == 0), stop=False)

            def low(b, m, gq):
                pe.wait_ge(eTl_ready, m + 3)
                for i in range(4):
                    t = gq * 4 + i
                    ins = mm(bk[3 - b][:, 256:512], eT[:, gq, 1, i * P:(i + 1) * P], yhl[:, b, t, 0, :],
                             start=False, stop=(t == NT - 1))
                ins.then_inc(comb_done, 1)

            def comb_batch1(j, m, first):
                def with_y(i):
                    if first:
                        pe.wait_ge(yl_ready, i + 1)
                with_y(0)
                high(1, 2 * j, m, 0)
                turn(1, j, m + 2, 2)
                if not first:
                    low(0, m - 1, 3)
                with_y(1)
                high(1, 2 * j, m + 1, 1)
                turn(1, j, m + 3, 3)
                low(1, m, 0)
                with_y(2)
                high(1, 2 * j, m + 2, 2)
                turn(0, j, m + 4, 0)
                low(1, m + 1, 1)
                with_y(3)
                high(1, 2 * j, m + 3, 3)
                low(1, m + 2, 2)

            def comb_pe(j, second):
                m = 8 * j
                def with_y(i):
                    if second:
                        pe.wait_ge(yl_ready, 4 + i + 1)
                turn(0, j - 1, m - 3, 1)
                low(1, m - 5, 3)
                if not second:
                    logits(j, range(4))
                with_y(0)
                high(0, 2 * j - 1, m - 4, 0)
                turn(0, j - 1, m - 2, 2)
                with_y(1)
                high(0, 2 * j - 1, m - 3, 1)
                turn(0, j - 1, m - 1, 3)
                low(0, m - 4, 0)
                with_y(2)
                high(0, 2 * j - 1, m - 2, 2)
                turn(1, j, m, 0)
                low(0, m - 3, 1)
                with_y(3)
                high(0, 2 * j - 1, m - 1, 3)
                turn(1, j, m + 1, 1)
                low(0, m - 2, 2)
                comb_batch1(j, m, False)

            def logits0(kb):
                pe.wait_ge(slots_evac, NB * 4 + kb + 1)
                logits(0, (kb,))

            logits0(0)
            logits0(1)
            for q in range(TB):
                y_product(NB - 1, q)
                if q < 2:
                    logits0(q + 2)
                else:
                    turn(1, 0, q - 2, q - 2)
                y_turn(NB - 1, q)
            pe.wait_ge(E1_ready, 2)
            pe.wait_ge(m0_ready, 1)
            logits(1, range(4))
            comb_batch1(0, 0, True)
            comb_pe(1, True)
            with pe.Fori(2, NJ) as j:
                comb_pe(j, False)
            m = 8 * NJ
            turn(0, NJ - 1, m - 3, 1)
            low(1, m - 5, 3)
            high(0, 2 * NJ - 1, m - 4, 0)
            turn(0, NJ - 1, m - 2, 2)
            high(0, 2 * NJ - 1, m - 3, 1)
            turn(0, NJ - 1, m - 1, 3)
            low(0, m - 4, 0)
            high(0, 2 * NJ - 1, m - 2, 2)
            low(0, m - 3, 1)
            high(0, 2 * NJ - 1, m - 1, 3)
            low(0, m - 2, 2)
            low(0, m - 1, 3)


def kernel(**inputs):
    import numpy as np
    import concourse.bacc as bacc
    from concourse.bass_utils import run_bass_kernel_spmd

    nc = bacc.Bacc("TRN2", target_bir_lowering=False, num_devices=1)
    laid = {
        "x": inputs["L0_attn_x"],
        "norm_w": inputs["L0_attn_norm_w"],
        "norm_b": inputs["L0_attn_norm_b"],
        "qkv_w": inputs["L0_attn_qkv_w"],
        "qkv_b": np.reshape(inputs["L0_attn_qkv_b"], (-1, 128)).T,
        "proj_wT": np.transpose(inputs["L0_attn_proj_w"]),
        "proj_b": inputs["L0_attn_proj_b"],
        "phi": inputs["L0_ffn_phi"],
        "ffn_w": inputs["L0_ffn_W"],
        "ffn_bT": np.transpose(inputs["L0_ffn_b"]),
    }
    arrays, args = {}, []
    for name, a in laid.items():
        a = np.ascontiguousarray(a)
        arrays[f"in_{name}"] = a
        args.append(nc.dram_tensor(f"in_{name}", a.shape, mybir.dt.from_np(a.dtype), kind="ExternalInput").ap())
    out = nc.dram_tensor("out", laid["x"].shape, F32, kind="ExternalOutput").ap()
    build(nc, *args, out)
    r = run_bass_kernel_spmd(nc, [arrays], core_ids=[0])
    return r.results[0]["out"]
```
